# Optimizing a Trainium2 kernel written in Bass

```python
import numpy as np
import jax
import jax.numpy as jnp

def _softmax(x, axis=-1):
    return jax.nn.softmax(x, axis=axis)

def _gelu(x):
    return jax.nn.gelu(x, approximate=True)

def _silu(x):
    return jax.nn.silu(x)

def _sigmoid(x):
    return jax.nn.sigmoid(x)

def _layernorm(x, axis=-1, eps=1e-05):
    m = jnp.mean(x, axis=axis, keepdims=True)
    v = jnp.var(x, axis=axis, keepdims=True)
    return (x - m) / jnp.sqrt(v + eps)

def _scatter_add(tgt, idx, src, axis=0):
    return tgt.at[idx].add(src)

def _segment_sum(src, seg, n):
    return jax.ops.segment_sum(src, seg, n)
kernel_name = 'mk_perceiver_d1_seqx_r8_e1b402'

def setup_inputs(seed: int=0):
    np.random.seed(seed)
    _w = jnp.asarray

    def _rec_inputs():
        import jax
        import jax.numpy as jnp
        _rk = jax.random.key(seed)
        x = -0.000929 + 1 * jax.random.normal(jax.random.fold_in(_rk, 1), (4, 128, 128), jnp.float32)
        _lenS = 128 - jax.random.randint(jax.random.fold_in(_rk, 7), (4,), 0, max(1, 128 // 4) + 1, jnp.int32)
        _lenS2 = 2048 - jax.random.randint(jax.random.fold_in(_rk, 8), (4,), 0, max(1, 2048 // 4) + 1, jnp.int32)
        _ctx_1024P = jax.random.normal(jax.random.fold_in(_rk, 11), (4, 16, 128), jnp.float32)
        _ctx_1024c = jax.random.dirichlet(jax.random.fold_in(_rk, 511), 0.3 * jnp.ones((16,), jnp.float32), (4, 2048))
        _ctx_1024t = jnp.einsum('bsk,bkd->bsd', _ctx_1024c, _ctx_1024P)
        _ctx_1024t = _ctx_1024t * jax.lax.rsqrt(jnp.mean(jnp.square(_ctx_1024t)) + 1e-12) * 0.953939
        ctx_1024 = 0.000227908 + 0.99994 * (_ctx_1024t + 0.3 * jax.random.normal(jax.random.fold_in(_rk, 611), (4, 2048, 128), jnp.float32))
        fside_BxSxS2_0 = jax.random.uniform(jax.random.fold_in(_rk, 12), (4, 128, 2048), jnp.float32, 0.0, 0.999998)
        _validS = jnp.arange(128)[None, :] < _lenS[:, None]
        _validS2 = jnp.arange(2048)[None, :] < _lenS2[:, None]
        _causal = jnp.tril(jnp.ones((128, 128), dtype=bool))
        mask_Bx1x1xS2_ff0 = jnp.where(jnp.ones((4, 1, 1, 2048), dtype=bool), 0.0, -1000000000.0).astype(jnp.float32)
        return (x, ctx_1024, fside_BxSxS2_0, mask_Bx1x1xS2_ff0)
    x, ctx_1024, fside_BxSxS2_0, mask_Bx1x1xS2_ff0 = _rec_inputs()

    def _L0_xattn_setup():
        import jax, jax.numpy as jnp
        import numpy as np
        B, F, T = (2, 64, 64)
        D, N, H = (128, 16, 64)
        K = 32
        FILT = 512
        L = 4
        EPS = 1e-06

        def _glorot(key, shape, fan_in, fan_out):
            lim = np.sqrt(6.0 / (fan_in + fan_out)).astype(np.float32)
            return jax.random.uniform(key, shape, jnp.float32, -lim, lim)

        def _norm(x):
            m = jnp.mean(x, axis=-1, keepdims=True)
            s = jnp.sqrt(jnp.mean((x - m) ** 2, axis=-1, keepdims=True))
            return (x - m) / (s + EPS)

        def _attention(x, src, dist, bias, Wq, Wk, Wv, Wo, Wth, bth, Wto, bto):
            q = jnp.einsum('bfd,dnh->bfnh', x, Wq) * H ** (-0.5)
            k = jnp.einsum('btd,dnh->btnh', src, Wk)
            v = jnp.einsum('btd,dnh->btnh', src, Wv)
            hbias = jax.nn.relu(dist[..., None] @ Wth + bth)
            qs_bias = (hbias @ Wto + bto)[..., 0]
            logits = jnp.einsum('btnh,bfnh->bnft', k, q)
            logits = logits + bias + qs_bias[:, None]
            w = jax.nn.softmax(logits, axis=-1)
            out = jnp.einsum('bnft,btnh->bfnh', w, v)
            return jnp.einsum('bfnh,nhd->bfd', out, Wo)
        key = jax.random.key(seed)
        ks = jax.random.split(key, 18)
        inp = {'decoder_inputs': jax.random.normal(ks[0], (B, F, D), jnp.float32), 'encoder_outputs': jax.random.normal(ks[1], (B, T, D), jnp.float32), 'decoder_times_dist': jax.random.uniform(ks[2], (B, F, F), jnp.float32), 'decoder_encoder_times_dist': jax.random.uniform(ks[3], (B, F, T), jnp.float32), 'dec_self_attn_bias': jnp.zeros((B, 1, 1, F), jnp.float32), 'enc_dec_attn_bias': jnp.zeros((B, 1, 1, T), jnp.float32), 'Wq': _glorot(ks[4], (L, D, N, H), D, D), 'Wk': _glorot(ks[5], (L, D, N, H), D, D), 'Wv': _glorot(ks[6], (L, D, N, H), D, D), 'Wo': _glorot(ks[7], (L, N, H, D), D, D), 'Wth': _glorot(ks[8], (L, 1, K), 1, K), 'bth': jnp.zeros((L, K), jnp.float32), 'Wto': _glorot(ks[9], (L, K, 1), K, 1), 'bto': jnp.zeros((L, 1), jnp.float32), 'Wf1': _glorot(ks[10], (L, D, FILT), D, FILT), 'bf1': jnp.zeros((L, FILT), jnp.float32), 'Wf2': _glorot(ks[11], (L, FILT, D), FILT, D), 'bf2': jnp.zeros((L, D), jnp.float32)}
        return inp
    _L0_xattn_all = _L0_xattn_setup()
    _L0_xattn_in = {k: v for k, v in _L0_xattn_all.items() if k in ('Wq', 'Wk', 'Wv', 'Wo', 'Wth', 'bth', 'Wto', 'bto', 'Wf1', 'bf1', 'Wf2', 'bf2')}
    del _L0_xattn_all

    def _L0_attn_setup():
        import jax, jax.numpy as jnp
        import numpy as np
        B, S, D, H = (2, 256, 128, 16)
        DK = D // H
        key = jax.random.key(seed)
        ks = jax.random.split(key, 9)
        s = 0.02
        return {'embeddings': jax.random.normal(ks[0], (B, S, D), jnp.float32), 'Wq': jax.random.normal(ks[1], (H, D, DK), jnp.float32) * s, 'bq': jax.random.normal(ks[2], (H, DK), jnp.float32) * s, 'Wk': jax.random.normal(ks[3], (H, D, DK), jnp.float32) * s, 'bk': jax.random.normal(ks[4], (H, DK), jnp.float32) * s, 'Wv': jax.random.normal(ks[5], (H, D, DK), jnp.float32) * s, 'bv': jax.random.normal(ks[6], (H, DK), jnp.float32) * s, 'Wo': jax.random.normal(ks[7], (D, D), jnp.float32) * s, 'bo': jax.random.normal(ks[8], (D,), jnp.float32) * s}
    _L0_attn_all = _L0_attn_setup()
    _L0_attn_in = {k: v for k, v in _L0_attn_all.items() if k in ('Wq', 'bq', 'Wk', 'bk', 'Wv', 'bv', 'Wo', 'bo')}
    del _L0_attn_all

    def _L0_ffn_setup():
        import jax, jax.numpy as jnp
        import numpy as np
        TOP_K = 2
        key = jax.random.key(seed)
        ks = jax.random.split(key, 6)
        B, S, H, F, E = (4, 256, 128, 512, 8)
        scale = 0.02
        x = jax.random.normal(ks[0], (B, S, H), dtype=jnp.float32)
        gate_w = jax.random.normal(ks[1], (E, H), dtype=jnp.float32) * scale
        w1 = jax.random.normal(ks[2], (E, H, F), dtype=jnp.float32) * scale
        b1 = jnp.zeros((E, F), dtype=jnp.float32)
        w2 = jax.random.normal(ks[3], (E, F, H), dtype=jnp.float32) * scale
        b2 = jnp.zeros((E, H), dtype=jnp.float32)
        return {'x': x, 'gate_w': gate_w, 'w1': w1, 'b1': b1, 'w2': w2, 'b2': b2}
    _L0_ffn_all = _L0_ffn_setup()
    _L0_ffn_in = {k: v for k, v in _L0_ffn_all.items() if k in ('gate_w', 'w1', 'b1', 'w2', 'b2')}
    del _L0_ffn_all
    return {'x': x, 'ctx_1024': ctx_1024, 'fside_BxSxS2_0': fside_BxSxS2_0, 'mask_Bx1x1xS2_ff0': mask_Bx1x1xS2_ff0, 'L0_xattn_Wq': _L0_xattn_in['Wq'], 'L0_xattn_Wk': _L0_xattn_in['Wk'], 'L0_xattn_Wv': _L0_xattn_in['Wv'], 'L0_xattn_Wo': _L0_xattn_in['Wo'], 'L0_xattn_Wth': _L0_xattn_in['Wth'], 'L0_xattn_bth': _L0_xattn_in['bth'], 'L0_xattn_Wto': _L0_xattn_in['Wto'], 'L0_xattn_bto': _L0_xattn_in['bto'], 'L0_xattn_Wf1': _L0_xattn_in['Wf1'], 'L0_xattn_bf1': _L0_xattn_in['bf1'], 'L0_xattn_Wf2': _L0_xattn_in['Wf2'], 'L0_xattn_bf2': _L0_xattn_in['bf2'], 'L0_attn_Wq': _L0_attn_in['Wq'], 'L0_attn_bq': _L0_attn_in['bq'], 'L0_attn_Wk': _L0_attn_in['Wk'], 'L0_attn_bk': _L0_attn_in['bk'], 'L0_attn_Wv': _L0_attn_in['Wv'], 'L0_attn_bv': _L0_attn_in['bv'], 'L0_attn_Wo': _L0_attn_in['Wo'], 'L0_attn_bo': _L0_attn_in['bo'], 'L0_ffn_gate_w': _L0_ffn_in['gate_w'], 'L0_ffn_w1': _L0_ffn_in['w1'], 'L0_ffn_b1': _L0_ffn_in['b1'], 'L0_ffn_w2': _L0_ffn_in['w2'], 'L0_ffn_b2': _L0_ffn_in['b2']}

def reference(x, ctx_1024, fside_BxSxS2_0, mask_Bx1x1xS2_ff0, L0_xattn_Wq, L0_xattn_Wk, L0_xattn_Wv, L0_xattn_Wo, L0_xattn_Wth, L0_xattn_bth, L0_xattn_Wto, L0_xattn_bto, L0_xattn_Wf1, L0_xattn_bf1, L0_xattn_Wf2, L0_xattn_bf2, L0_attn_Wq, L0_attn_bq, L0_attn_Wk, L0_attn_bk, L0_attn_Wv, L0_attn_bv, L0_attn_Wo, L0_attn_bo, L0_ffn_gate_w, L0_ffn_w1, L0_ffn_b1, L0_ffn_w2, L0_ffn_b2):
    import jax
    import jax.numpy as jnp

    def _L0_xattn_ref(decoder_inputs, encoder_outputs, decoder_times_dist, decoder_encoder_times_dist, dec_self_attn_bias, enc_dec_attn_bias, Wq, Wk, Wv, Wo, Wth, bth, Wto, bto, Wf1, bf1, Wf2, bf2):
        import jax, jax.numpy as jnp
        import numpy as np
        B, F, T = (2, 64, 64)
        D, N, H = (128, 16, 64)
        K = 32
        FILT = 512
        L = 4
        EPS = 1e-06

        def _glorot(key, shape, fan_in, fan_out):
            lim = np.sqrt(6.0 / (fan_in + fan_out)).astype(np.float32)
            return jax.random.uniform(key, shape, jnp.float32, -lim, lim)

        def _norm(x):
            m = jnp.mean(x, axis=-1, keepdims=True)
            s = jnp.sqrt(jnp.mean((x - m) ** 2, axis=-1, keepdims=True))
            return (x - m) / (s + EPS)

        def _attention(x, src, dist, bias, Wq, Wk, Wv, Wo, Wth, bth, Wto, bto):
            q = jnp.einsum('bfd,dnh->bfnh', x, Wq) * H ** (-0.5)
            k = jnp.einsum('btd,dnh->btnh', src, Wk)
            v = jnp.einsum('btd,dnh->btnh', src, Wv)
            hbias = jax.nn.relu(dist[..., None] @ Wth + bth)
            qs_bias = (hbias @ Wto + bto)[..., 0]
            logits = jnp.einsum('btnh,bfnh->bnft', k, q)
            logits = logits + bias + qs_bias[:, None]
            w = jax.nn.softmax(logits, axis=-1)
            out = jnp.einsum('bnft,btnh->bfnh', w, v)
            return jnp.einsum('bfnh,nhd->bfd', out, Wo)
        x = decoder_inputs
        for i in range(L):
            y = _attention(_norm(x), encoder_outputs, decoder_encoder_times_dist, enc_dec_attn_bias, Wq[i], Wk[i], Wv[i], Wo[i], Wth[i], bth[i], Wto[i], bto[i])
            x = x + y
            y = jax.nn.relu(_norm(x) @ Wf1[i] + bf1[i]) @ Wf2[i] + bf2[i]
            x = x + y
        return _norm(x)

    def _L0_attn_ref(embeddings, Wq, bq, Wk, bk, Wv, bv, Wo, bo):
        import jax, jax.numpy as jnp
        import numpy as np
        B, S, D, H = (2, 256, 128, 16)
        DK = D // H
        b, s, d = embeddings.shape
        dk = Wq.shape[-1]
        q = jnp.einsum('bsd,hdk->bhsk', embeddings, Wq) + bq[None, :, None, :]
        k = jnp.einsum('bsd,hdk->bhsk', embeddings, Wk) + bk[None, :, None, :]
        v = jnp.einsum('bsd,hdk->bhsk', embeddings, Wv) + bv[None, :, None, :]
        scores = jnp.einsum('bhqk,bhsk->bhqs', q, k) / jnp.sqrt(jnp.float32(dk))
        causal_mask = jnp.triu(jnp.ones((s, s), dtype=bool), k=1)
        scores = jnp.where(causal_mask, jnp.float32(-1000000000.0), scores)
        weights = jax.nn.softmax(scores, axis=-1)
        ctx = jnp.einsum('bhqs,bhsk->bhqk', weights, v)
        concat = ctx.transpose(0, 2, 1, 3).reshape(b, s, d)
        return concat @ Wo + bo

    def _L0_ffn_ref(x, gate_w, w1, b1, w2, b2):
        import jax, jax.numpy as jnp
        import numpy as np
        TOP_K = 2
        E = gate_w.shape[0]
        gate_logits = jnp.einsum('bsh,eh->bse', x, gate_w)
        gate_probs = jax.nn.softmax(gate_logits, axis=-1)
        top_v, top_i = jax.lax.top_k(gate_probs, TOP_K)
        onehot = jax.nn.one_hot(top_i, E, dtype=x.dtype)
        comb_w = jnp.einsum('bsk,bske->bse', top_v, onehot)
        out = jnp.zeros_like(x)
        for e in range(E):
            h = jax.nn.silu(jnp.einsum('bsh,hf->bsf', x, w1[e]) + b1[e])
            y = jnp.einsum('bsf,fh->bsh', h, w2[e]) + b2[e]
            out = out + y * comb_w[..., e:e + 1]
        return out
    x = x + _L0_xattn_ref(_layernorm(x, axis=-1), ctx_1024, fside_BxSxS2_0, fside_BxSxS2_0, mask_Bx1x1xS2_ff0, mask_Bx1x1xS2_ff0, L0_xattn_Wq, L0_xattn_Wk, L0_xattn_Wv, L0_xattn_Wo, L0_xattn_Wth, L0_xattn_bth, L0_xattn_Wto, L0_xattn_bto, L0_xattn_Wf1, L0_xattn_bf1, L0_xattn_Wf2, L0_xattn_bf2)
    x = x + _L0_attn_ref(_layernorm(x, axis=-1), L0_attn_Wq, L0_attn_bq, L0_attn_Wk, L0_attn_bk, L0_attn_Wv, L0_attn_bv, L0_attn_Wo, L0_attn_bo)
    x = x + _L0_ffn_ref(_layernorm(x, axis=-1), L0_ffn_gate_w, L0_ffn_w1, L0_ffn_b1, L0_ffn_w2, L0_ffn_b2)
    return x

_drawn_inputs = setup_inputs


def setup_inputs(seed=0):
    import zlib

    import numpy as np

    out = dict(_drawn_inputs(seed))
    spreads = {'L0_xattn_bth': (0.0, 0.8),
     'L0_xattn_bto': (0.0, 0.8),
     'L0_xattn_bf1': (0.0, 0.1),
     'L0_xattn_bf2': (0.0, 0.1),
     'L0_ffn_b1': (0.0, 0.8),
     'L0_ffn_b2': (0.0, 0.549)}
    factors = {'fside_BxSxS2_0': 8.0,
     'L0_xattn_Wth': 8.0,
     'L0_xattn_Wto': 8.0,
     'L0_attn_Wq': 8.0,
     'L0_attn_bq': 8.0,
     'L0_attn_Wk': 8.0,
     'L0_attn_bk': 8.0,
     'L0_attn_Wv': 3.008,
     'L0_attn_bv': 8.0,
     'L0_attn_Wo': 3.2,
     'L0_attn_bo': 4.338,
     'L0_ffn_gate_w': 4.058,
     'L0_ffn_w1': 7.346,
     'L0_ffn_w2': 6.71}
    for name, (base, spread) in spreads.items():
        noise = np.random.default_rng([zlib.crc32(name.encode()), seed]).standard_normal(out[name].shape)
        drawn = base * np.exp(spread * noise) if base else spread * noise
        out[name] = jnp.asarray(drawn.astype(out[name].dtype))
    for name, factor in factors.items():
        out[name] = (out[name] * factor).astype(out[name].dtype)
    return out
```

```python
from contextlib import ExitStack

import concourse.bass as bass
from concourse import mybir

F32 = mybir.dt.float32
F16 = mybir.dt.float16
ALU = mybir.AluOpType
ACT = mybir.ActivationFunctionType
AX = mybir.AxisListType

B, F, D = 4, 128, 128
T = 2048
L, NH, HD = 4, 16, 64
K = 32
FILT = 512
NB = T // 128
FC = FILT // 128
STEPS = L * B
NORM_EPS = 1e-6
Q_UP = 64.0
LN_EPS = 1e-5
NE = 8
SH, SK = 16, 8
NEG = -1.0e9
LOW = -3.0e38

FIRST, MID, LAST = 0, 1, 2

SMALL = {
    FIRST: {0: "v", 2: "v", 4: "v", 5: "v", 7: "v", 8: "v", 9: "v", 11: "v", 12: "v", 13: "v", 15: "v"},
    MID: {0: "v", 1: "v", 2: "v", 3: "v", 4: "v", 5: "v", 6: "v", 7: "v", 8: "v", 9: "v", 10: "a",
          11: "v", 12: "v", 13: "v", 14: "v", 15: "v"},
    LAST: {0: "v", 1: "v", 3: "v", 5: "v", 6: "v", 7: "v", 9: "v", 10: "a", 11: "v", 13: "v", 14: "v",
           15: "v", 17: "v", 19: "v", 20: "v", 21: "a", 22: "v"},
}
QUERY_SLOTS = (4, 8, 12, 0)
LAST_SLOTS = 23


def snap(eng, value):
    return value if isinstance(value, int) else eng.snap(value)


def small_count(kind, s, slot, who="av"):
    def n(k, upto=99):
        return sum(1 for j, w in SMALL[k].items() if w in who and j <= upto)
    if kind == FIRST:
        return n(FIRST, slot)
    if kind == MID:
        return (s - 1) * n(MID) + (n(FIRST) + n(MID, slot))
    return n(FIRST) + (STEPS - 2) * n(MID) + n(LAST, slot)


def by_engine(kind, s, slot):
    own = [j for j in SMALL[kind] if j < slot]
    if own:
        j = max(own)
        return SMALL[kind][j], small_count(kind, s, j, SMALL[kind][j])
    if kind == FIRST:
        return None, 0
    w = SMALL[MID][15]
    return w, small_count(kind, s, -1, w)


CHUNKS_A, CHUNKS_V = 3 * NH + NH // 2, NH // 2


def chunks_a(s, slot, c):
    assert c < 3 or slot % 2 == 1
    return s * CHUNKS_A + (3 * (slot - 1) + slot // 2 + c + 1)


def chunks_v(s, slot):
    assert slot % 2 == 0
    return s * CHUNKS_V + slot // 2


def perceiver(nc, a, out):
    xq, xk, xv, xo = (a["L0_xattn_" + n] for n in ("Wq", "Wk", "Wv", "Wo"))
    score_dram = nc.dram_tensor("score_weights", (L, 128, NH, 128), F32, kind="Internal").ap()
    value_dram = nc.dram_tensor("value_weights", (L, 128, NH, 128), F32, kind="Internal").ap()
    x_dram = a["x"].rearrange("b f d -> f b d")
    ctx_dram = a["ctx_1024"].rearrange("b (k p) d -> b p k d", p=128)
    side_dram = a["fside_BxSxS2_0"]
    mask_dram = a["mask_Bx1x1xS2_ff0"].rearrange("b o n t -> (b o n) t")

    with ExitStack() as top:
        def sem(name):
            return top.enter_context(nc.semaphore(name))

        def sbuf(ctx, name, shape, dtype=F32):
            return ctx.enter_context(nc.sbuf_tensor(name, shape, dtype))

        def psum(ctx, name, shape):
            return ctx.enter_context(nc.psum_tensor(name, shape, F32))

        x_all = sbuf(top, "x_all", [128, B, D])
        ident = sbuf(top, "ident", [128, 128])
        ones = sbuf(top, "ones", [128, 128])
        half = sbuf(top, "half", [128, 3])
        stats = sbuf(top, "stats", [128, B, 6])
        moments = sbuf(top, "moments", [128, B, 2])
        dev = sbuf(top, "dev", [128, B])
        rdev = sbuf(top, "rdev", [128, B])

        with ExitStack() as mem:
            cross_attention(nc, a, top, mem, sem, sbuf, psum, locals())
        with ExitStack() as mem:
            self_attention_and_experts(nc, a, out, top, mem, sem, sbuf, psum, locals())


def cross_attention(nc, a, top, mem, sem, sbuf, psum, g_):
    x_all, ident, ones, half = g_["x_all"], g_["ident"], g_["ones"], g_["half"]
    stats, moments, dev, rdev = g_["stats"], g_["moments"], g_["dev"], g_["rdev"]
    score_dram, value_dram, x_dram = g_["score_dram"], g_["value_dram"], g_["x_dram"]
    ctx_dram, side_dram, mask_dram = g_["ctx_dram"], g_["side_dram"], g_["mask_dram"]

    ctx_t = sbuf(mem, "ctx_t", [128, 2, B * T], F16)
    side = sbuf(mem, "side", [128, B * T])
    ctx_n = sbuf(mem, "ctx_n", [128, NB, 128])
    q_t = sbuf(mem, "q_t", [128, 2, NH, 128], F16)
    w_score = sbuf(mem, "w_score", [128, NH, 128])
    w_value = sbuf(mem, "w_value", [128, NH, 128])
    bias = sbuf(mem, "bias", [128, T])
    bias_sum = sbuf(mem, "bias_sum", [128, T])
    unit = sbuf(mem, "unit", [128, 2, T])
    mask = sbuf(mem, "mask", [128, T])
    gw_all = sbuf(mem, "gw_all", [128, L * 4 * K])
    gw_act = sbuf(mem, "gw_act", [128, 2 * K])
    gw_dve = sbuf(mem, "gw_dve", [128, K])
    gw_pool = sbuf(mem, "gw_pool", [128, 1])
    x_t = sbuf(mem, "x_t", [128, 128])
    x_n = sbuf(mem, "x_n", [128, 128])
    x_now = sbuf(mem, "x_now", [128, 128])

    unit_ready, bias_added = sem("unit_ready"), sem("bias_added")
    mask_loaded, mask_summed, mask_ready = sem("mask_loaded"), sem("mask_summed"), sem("mask_ready")

    prologue(nc, a, mem, sem, sbuf, psum, {**g_, **locals()})

    probs = sbuf(mem, "probs", [128, 2, T])
    probs_t = sbuf(mem, "probs_t", [128, 2, NB * 256])
    mix_t = sbuf(mem, "mix_t", [128, 256])
    y_sum = sbuf(mem, "y_sum", [128, 128])
    x_mid = sbuf(mem, "x_mid", [128, 128])
    f_n = sbuf(mem, "f_n", [128, 128])
    f_t = sbuf(mem, "f_t", [128, 128])
    hid_t = sbuf(mem, "hid_t", [128, FILT])
    wf1 = sbuf(mem, "wf1", [128, FILT])
    wf2 = sbuf(mem, "wf2", [128, FC, 128])
    bf1 = sbuf(mem, "bf1", [1, FILT])
    bf2 = sbuf(mem, "bf2", [1, 128])
    tops = sbuf(mem, "tops", [128, 2])
    negmax = sbuf(mem, "negmax", [128, 2])
    sums = sbuf(mem, "sums", [128, NH])
    rsum = sbuf(mem, "rsum", [128, 2])
    mom = sbuf(mem, "mom", [128, 2, 2])
    st = sbuf(mem, "st", [128, 2, 6])
    sd = sbuf(mem, "sd", [128, 2])
    rs = sbuf(mem, "rs", [128, 2])
    pace = sbuf(mem, "pace", [128, 4])

    ps_s = psum(mem, "ps_s", [128, T])
    ps_t = psum(mem, "ps_t", [128, 2, 512])
    ps_u = psum(mem, "ps_u", [128, 512])
    ps_m = psum(mem, "ps_m", [128, 512])

    scored = sem("scored")
    taken = sem("taken")
    max_ready = sem("max_ready")
    exp_ready = sem("exp_ready")
    turned = sem("turned")
    turned_out_a = sem("turned_out_a")
    turned_out_v = sem("turned_out_v")
    mixing = sem("mixing")
    mix_out = sem("mix_out")
    small = sem("small")
    small_out_a, small_out_v = sem("small_out_a"), sem("small_out_v")
    upper_ready = sem("upper_ready")
    y_added = sem("y_added")
    xn_ready = sem("xn_ready")
    fn_ready = sem("fn_ready")
    mom_ready = sem("mom_ready")
    sd_ready = sem("sd_ready")
    bto_here = sem("bto_here")
    dve_step = sem("dve_step")
    gw_act_ready, gw_dve_ready = sem("gw_act_ready"), sem("gw_dve_ready")
    w_score_in, w_value_in = sem("w_score_in"), sem("w_value_in")
    ctx_lo_in, ctx_hi_in, ffn_in = sem("ctx_lo_in"), sem("ctx_hi_in"), sem("ffn_in")

    def at(s, per, off):
        return s * per + off

    def steps(eng, body):
        body(FIRST, 0)
        with eng.Fori(1, STEPS - 1) as s:
            body(MID, s)
        body(LAST, STEPS - 1)

    def slots(kind):
        return range(LAST_SLOTS if kind == LAST else NH)

    block = mem.enter_context(nc.Block())

    @block.sync
    def _(sp):
        def body(kind, s):
            if kind != FIRST:
                sp.wait_ge(small, small_count(kind, s, -1))
                lay = snap(sp, (s - 1) // B)
                sp.dma_start(wf1[:, :], a["L0_xattn_Wf1"][bass.ds(lay, 1), :, :].rearrange("l d n -> d (l n)")).then_inc(ffn_in, 16)
                sp.dma_start(wf2[:, :, :], a["L0_xattn_Wf2"][bass.ds(lay, 1), :, :].rearrange("l (c p) d -> p (l c) d", p=128)).then_inc(ffn_in, 16)
                sp.dma_start(bf1[:, :], a["L0_xattn_bf1"][bass.ds(lay, 1), :]).then_inc(ffn_in, 16)
                sp.dma_start(bf2[:, :], a["L0_xattn_bf2"][bass.ds(lay, 1), :]).then_inc(ffn_in, 16)
            if kind == MID:
                sp.wait_ge(small, small_count(kind, s, 0))
                lay = snap(sp, (s + 1) // B)
                sp.dma_start(w_score[:, :, :], score_dram[bass.ds(lay, 1)].rearrange("l p n d -> p (l n) d")).then_inc(w_score_in, 16)
            if kind != LAST:
                sp.wait_ge(bias_added, at(s, K, K + 1))
                b2 = snap(sp, (s + 2) % B)
                sp.dma_start(mask[:, :], mask_dram[bass.ds(b2, 1), :].to_broadcast([128, T])).then_inc(mask_loaded, 16)
            if kind != FIRST:
                b0 = snap(sp, s % B)
                sp.wait_ge(mixing, at(s, NH, -1))
                sp.dma_start(ctx_n[:, 0:NB // 2, :], ctx_dram[bass.ds(b0, 1), :, 0:NB // 2, :].rearrange("b p k d -> p (b k) d")).then_inc(ctx_lo_in, 16)
                sp.wait_ge(mixing, at(s, NH, 0))
                sp.dma_start(ctx_n[:, NB // 2:NB, :], ctx_dram[bass.ds(b0, 1), :, NB // 2:NB, :].rearrange("b p k d -> p (b k) d")).then_inc(ctx_hi_in, 16)
                sp.wait_ge(small, small_count(kind, s, 3))
                lay = snap(sp, s // B)
                sp.dma_start(w_value[:, :, :], value_dram[bass.ds(lay, 1)].rearrange("l p n d -> p (l n) d")).then_inc(w_value_in, 16)

        steps(sp, body)

    @block.gpsimd
    def _(pool):
        def body(kind, s):
            if kind != LAST:
                n = 1 if kind == FIRST else at(s, 2, 0)
                pool.wait_ge(mom_ready, n)
                pool.tensor_tensor(sd[:, 0:1], mom[:, 0, 1:2], half[:, 0:1], ALU.pow).then_inc(sd_ready, 1)
                lay = snap(pool, ((s + 2) % STEPS) // B)
                pool.tensor_copy(gw_pool[:, :], gw_all[:, bass.ds(lay * (4 * K) + 3 * K, 1)]).then_inc(bto_here, 1)
                pool.wait_ge(bto_here, at(s, 1, 1))
                pool.wait_ge(mask_loaded, at(s, 16, 48))
                pool.tensor_tensor(mask[:, :], mask[:, :], gw_pool[:, 0:1].to_broadcast([128, T]), ALU.add).then_inc(mask_summed, 1)
                pool.wait_ge(mask_summed, at(s, 1, 3))
                pool.tensor_tensor(mask[:, :], mask[:, :], half[:, 2:3].to_broadcast([128, T]), ALU.mult).then_inc(mask_ready, 1)
            if kind != FIRST:
                n = at(s, 2, 1) if kind == MID else 2 * s
                pool.wait_ge(mom_ready, n)
                pool.tensor_tensor(sd[:, 1:2], mom[:, 1, 1:2], half[:, 0:1], ALU.pow).then_inc(sd_ready, 1)
            if kind == LAST:
                pool.wait_ge(mom_ready, 2 * s + 1)
                pool.tensor_tensor(sd[:, 1:2], mom[:, 1, 1:2], half[:, 0:1], ALU.pow).then_inc(sd_ready, 1)

        steps(pool, body)

    @block.tensor
    def _(pe):
        def take_small(kind, s, slot):
            who, n = by_engine(kind, s, slot)
            if who is not None:
                pe.wait_ge(small_out_a if who == "a" else small_out_v, n)

        def scores(kind, s, j):
            if j == 12:
                pe.wait_ge(small_out_v, small_count(kind, s, 0, "v"))
            elif j == 0 and kind != FIRST:
                pe.wait_ge(small_out_v, small_count(kind, s, -1, "v"))
            bcol = snap(pe, (s % B) * T)
            for h in range(2):
                if not (kind == FIRST and j == 0):
                    pe.wait_ge(taken, at(s, 2 * NH, 2 * j - 1 + h))
                for q_part, c_part, c in ((0, 0, 0), (0, 1, 0), (0, 0, 1), (0, 1, 1), (1, 0, 0), (1, 0, 1)):
                    lo = (2 * h + c) * 512
                    mm = pe.matmul(ps_s[:, lo:lo + 512], q_t[:, q_part, j, :],
                                   ctx_t[:, c_part, bass.ds(bcol + lo, 512)],
                                   start=(q_part, c_part) == (0, 0), stop=q_part == 1)
                mm.then_inc(scored, 1)

        def turn(kind, s, j, c):
            if c == 0:
                pe.wait_ge(exp_ready, at(s, NH, j))
            first = kind == FIRST and j == 1
            if c == 0 and not first:
                pe.wait_ge(turned_out_a, chunks_a(s, j - 1, 2))
            if c == 1 and not first:
                if j % 2 == 0:
                    pe.wait_ge(turned_out_a, chunks_a(s, j - 1, 3))
                else:
                    pe.wait_ge(turned_out_v, chunks_v(s, j - 1))
            if c >= 2:
                pe.wait_ge(turned_out_a, chunks_a(s, j, c - 2))
            for i in range(4):
                k = 4 * c + i
                mm = pe.transpose(ps_t[:, c % 2, i * 128:(i + 1) * 128],
                                  probs[:, (j + 1) % 2, k * 128:(k + 1) * 128], ident[:, :])
            mm.then_inc(turned, 1)

        def mix(kind, s, j, i):
            lower = j % 2 == 1
            par = ((j - 3 if lower else j - 4) // 2) % 2
            if i == 0:
                head = j - 3 if lower else j - 4
                if lower:
                    pe.wait_ge(turned_out_a, chunks_a(s, head + 2, 1))
                    if not (kind == FIRST and j == 3):
                        pe.wait_ge(mix_out, at(s, NH // 2, head // 2))
                    if kind != FIRST and j == 3:
                        pe.wait_ge(ctx_lo_in, at(s, 16, 0))
                else:
                    pe.wait_ge(turned_out_a, chunks_a(s, head + 2, 2))
                    pe.wait_ge(turned_out_v, chunks_v(s, head + 2))
                    if kind != FIRST and j == 4:
                        pe.wait_ge(ctx_hi_in, at(s, 16, 0))
            for k in (2 * i, 2 * i + 1):
                k += 0 if lower else NB // 2
                mm = pe.matmul(ps_u[:, 0:256], ctx_n[:, k, :], probs_t[:, par, k * 256:(k + 1) * 256],
                               start=k == 0, stop=k == NB - 1)
            if i == 3:
                mm.then_inc(mixing, 1)

        def project(kind, s, j):
            head = j - 5
            pe.wait_ge(mix_out, at(s, NH // 2, head // 2 + 1))
            if kind != FIRST and j == 5:
                pe.wait_ge(w_value_in, at(s, 16, 0))
            for i in range(2):
                mm = pe.matmul(ps_m[:, i * 128:(i + 1) * 128], mix_t[:, i * 128:(i + 1) * 128],
                               w_value[:, (head + i) % NH, :], start=True, stop=True)
            mm.then_inc(small, 1)

        def queries(kind, s, j, group):
            if kind == MID and j == 4:
                pe.wait_ge(w_score_in, at(s, 16, 0))
            if j == 4:
                pe.wait_ge(small_out_v, small_count(kind, s, 2, "v"))
            for i in range(4):
                mm = pe.matmul(ps_m[:, i * 128:(i + 1) * 128], w_score[:, 4 * group + i, :], x_t[:, :],
                               start=True, stop=True)
            mm.then_inc(small, 1)

        def small_product(kind, s, j):
            if j not in SMALL[kind]:
                return
            take_small(kind, s, j)
            if j % 2 == 1 and j < 20:
                project(kind, s, j)
            elif j == 0:
                queries(kind, s, j, 3)
            elif j in (4, 8, 12):
                queries(kind, s, j, j // 4 - 1)
            elif j == 2:
                pe.wait_ge(xn_ready, at(s, 1, 1))
                pe.transpose(ps_m[:, 0:128], x_n[:, :], ident[:, :]).then_inc(small, 1)
            elif j in (6, 20):
                pe.wait_ge(fn_ready, s + (j == 20))
                pe.transpose(ps_m[:, 0:128], f_n[:, :], ident[:, :]).then_inc(small, 1)
            elif j in (10, 21):
                pe.wait_ge(ffn_in, at(s, 64, 0))
                pe.wait_ge(small_out_v, small_count(kind, s, 6 if j == 10 else 20, "v"))
                for c in range(FC):
                    o = ps_m[:, c * 128:(c + 1) * 128]
                    pe.matmul(o, wf1[:, c * 128:(c + 1) * 128], f_t[:, :], start=c == 0, stop=False,
                              skip_group_check=True)
                for c in range(FC):
                    mm = pe.matmul(ps_m[:, c * 128:(c + 1) * 128], bf1[0:1, c * 128:(c + 1) * 128], ones[0:1, :],
                                   start=False, stop=True, skip_group_check=True)
                mm.then_inc(small, 1)
            elif j in (14, 22):
                pe.wait_ge(small_out_a, small_count(kind, s, 10 if j == 14 else 21, "a"))
                for c in range(FC):
                    pe.matmul(ps_m[:, 0:128], hid_t[:, c * 128:(c + 1) * 128], wf2[:, c, :], start=c == 0, stop=False)
                pe.matmul(ps_m[:, 0:128], ones[0:1, :], bf2[0:1, :], start=False, stop=True).then_inc(small, 1)

        def body(kind, s):
            for j in slots(kind):
                if j < NH:
                    scores(kind, s, j)
                for i in range(4):
                    if (kind != FIRST or j >= 1) and j <= NH:
                        turn(kind, s, j, i)
                    if (kind != FIRST or j >= 3) and j <= NH + 2:
                        mix(kind, s, j, i)
                    if i == 1:
                        small_product(kind, s, j)

        steps(pe, body)

    @block.scalar
    def _(act):
        def unit_of(kind, s, nxt, k):
            n = at(s, K, nxt * K + k)
            bcol = snap(act, ((s + nxt) % B) * T)
            act.activation(unit[:, k % 2, :], side[:, bass.ds(bcol, T)], ACT.Relu,
                           scale=gw_act[:, k:k + 1], bias=gw_act[:, K + k:K + k + 1]).then_inc(unit_ready, 1)

        def chunk_out(kind, s, j, c, extra=()):
            for x_sem, v in extra:
                act.wait_ge(x_sem, v)
            act.wait_ge(turned, at(s, 4 * NH, 4 * (j - 1) + c + 1))
            dst = probs_t[:, ((j + 1) // 2 + 1) % 2, :].rearrange("p (k h f) -> p k h f", k=NB, h=2)
            act.activation(dst[:, 4 * c:4 * c + 4, (j + 1) % 2, :],
                           ps_t[:, c % 2, :].rearrange("p (k f) -> p k f", k=4), ACT.Copy).then_inc(turned_out_a, 1)

        def body(kind, s):
            for j in slots(kind):
                turning = (kind != FIRST or j >= 1) and j <= NH
                more = kind != LAST
                free = [(bias_added, at(s, K, K + 2 * j))] if more else []
                if turning:
                    chunk_out(kind, s, j, 0, free)
                elif free:
                    act.wait_ge(*free[0])
                if more:
                    unit_of(kind, s, 1, 2 * j + 1)
                if turning:
                    chunk_out(kind, s, j, 1)
                if more and j == NH - 1:
                    act.wait_ge(unit_ready, at(s, K, 2 * K))
                if j < NH:
                    act.wait_ge(max_ready, at(s, NH, j + 1))
                    act.activation(probs[:, j % 2, :], probs[:, j % 2, :], ACT.Exp, bias=negmax[:, j % 2:j % 2 + 1],
                                   accum_out=sums[:, j:j + 1]).then_inc(exp_ready, 1)
                if more and j == NH - 1:
                    lay = snap(act, ((s + 2) % STEPS) // B)
                    act.activation(gw_act[:, :], gw_all[:, bass.ds(lay * (4 * K), 2 * K)], ACT.Copy).then_inc(gw_act_ready, 1)
                if j in SMALL[kind] and (SMALL[kind][j] == "a" or j in QUERY_SLOTS):
                    act.wait_ge(small, small_count(kind, s, j))
                    if j in (10, 21):
                        act.activation(hid_t[:, :], ps_m[:, :], ACT.Relu).then_inc(small_out_a, 1)
                    else:
                        group = QUERY_SLOTS.index(j)
                        act.activation(q_t[:, 0, 4 * group:4 * group + 4, :],
                                       ps_m[:, :].rearrange("p (n f) -> p n f", n=4), ACT.Copy).then_inc(upper_ready, 1)
                free = [(bias_added, at(s, K, K + 2 * j + 1))] if more else []
                if more and j == NH - 1:
                    free.append((gw_act_ready, at(s, 1, 1)))
                if turning:
                    chunk_out(kind, s, j, 2, free)
                elif free:
                    act.wait_ge(*free[0])
                if more:
                    unit_of(kind, s, 1 if j < NH - 1 else 2, (2 * j + 2) % K)
                if turning and j % 2 == 1:
                    chunk_out(kind, s, j, 3)
                if j % 2 == 0 and (kind != FIRST or j >= 4) and j <= NH + 2:
                    act.wait_ge(mixing, at(s, NH, j - 2))
                    act.activation(mix_t[:, :], ps_u[:, 0:256], ACT.Copy).then_inc(mix_out, 1)

        steps(act, body)

    @block.vector
    def _(dve):
        TOTALS = 5 + 2 * 6, 5 + 2 * 8 + 4

        def body(kind, s):
            done = [0]
            total_first, total_mid = TOTALS

            def count():
                if kind == FIRST:
                    return done[0]
                if kind == MID:
                    return (s - 1) * total_mid + (total_first + done[0])
                return total_first + (STEPS - 2) * total_mid + done[0]

            def chain(ins):
                ins.then_inc(dve_step, 1)
                done[0] += 1
                return ins

            def settle():
                dve.wait_ge(dve_step, count())

            def normalise(w, src, dst, ready):
                chain(dve.tensor_scalar(rs[:, w:w + 1], sd[:, w:w + 1], NORM_EPS, None, ALU.add))
                settle()
                chain(dve.reciprocal(rs[:, w:w + 1], rs[:, w:w + 1]))
                settle()
                dve.tensor_scalar(dst[:, :], src[:, :], mom[:, w, 0:1], rs[:, w:w + 1],
                                  ALU.subtract, ALU.mult).then_inc(ready, 1)

            def add_unit(k):
                dve.wait_ge(unit_ready, at(s, K, K + k + 1))
                dve.wait_ge(bias_added, at(s, K, K + k))
                if k == 0:
                    dve.wait_ge(mask_ready, at(s, 1, 2))
                dve.scalar_tensor_tensor(out=(bias if k == K - 1 else bias_sum)[:, :], in0=unit[:, k % 2, :],
                                         scalar=gw_dve[:, k:k + 1], in1=(mask if k == 0 else bias_sum)[:, :],
                                         op0=ALU.mult, op1=ALU.add).then_inc(bias_added, 1)

            def moments_of(w, rows, column):
                chain(dve.bn_stats(st[:, w, :], rows[:, :]))
                settle()
                dve.memset(pace[:, column:column + 1], 0.0)
                dve.bn_aggr(mom[:, w, :], st[:, w, :]).then_inc(mom_ready, 1)

            def add_head(j, i):
                head = (j - 5) % NH
                src = ps_m[:, i * 128:(i + 1) * 128]
                settle()
                dve.wait_ge(small, small_count(kind, s, j))
                if i == 1:
                    dve.scalar_tensor_tensor(out=y_sum[:, :], in0=src, scalar=rsum[:, 1:2],
                                             in1=y_sum[:, :], op0=ALU.mult, op1=ALU.add).then_inc(small_out_v, 1)
                elif head == 0:
                    chain(dve.tensor_scalar(y_sum[:, :], src, rsum[:, 0:1], None, ALU.mult))
                else:
                    chain(dve.scalar_tensor_tensor(out=y_sum[:, :], in0=src, scalar=rsum[:, 0:1],
                                                   in1=y_sum[:, :], op0=ALU.mult, op1=ALU.add))

            for j in slots(kind):
                with_small = SMALL[kind].get(j) == "v"
                adds_heads = with_small and j % 2 == 1 and j < 20
                if adds_heads:
                    head = (j - 5) % NH
                    dve.wait_ge(exp_ready, at(s, NH, j - 3))
                    if j != 5 or kind != FIRST:
                        dve.wait_ge(small_out_v, small_count(kind, s, j - 1, "v"))
                    chain(dve.reciprocal(rsum[:, :], sums[:, head:head + 2]))
                if j < NH:
                    for h in range(2):
                        if h == 0 and not (kind == FIRST and j < 2):
                            dve.wait_ge(turned, at(s, 4 * NH, 4 * j - 4))
                        dve.wait_ge(scored, at(s, 2 * NH, 2 * j + 1 + h))
                        if h == 0 and not (kind == FIRST and j == 0):
                            dve.wait_ge(max_ready, at(s, NH, j))
                        if h == 0 and j == 0 and kind != FIRST:
                            dve.wait_ge(bias_added, at(s, K, K))
                        dve.memset(pace[:, h:h + 1], 0.0)
                        lo, hi = h * (T // 2), (h + 1) * (T // 2)
                        dve.tensor_tensor_reduce(probs[:, j % 2, lo:hi], ps_s[:, lo:hi], bias[:, lo:hi], 1.0 / Q_UP, LOW,
                                                 ALU.add, ALU.max, tops[:, h:h + 1]).then_inc(taken, 1)
                    dve.wait_ge(taken, at(s, 2 * NH, 2 * j + 2))
                    dve.tensor_scalar(negmax[:, j % 2:j % 2 + 1], tops[:, 0:1], tops[:, 1:2], -1.0,
                                      ALU.max, ALU.mult).then_inc(max_ready, 1)
                if kind != LAST and j == 0:
                    lay = snap(dve, ((s + 1) % STEPS) // B)
                    chain(dve.tensor_scalar(gw_dve[:, :], gw_all[:, bass.ds(lay * (4 * K) + 2 * K, K)], 1.0, None,
                                            ALU.mult))
                    bn = snap(dve, ((s + 1) % B) * D)
                    chain(dve.tensor_scalar(x_now[:, :], x_all[:, :, :].rearrange("p b d -> p (b d)")[:, bass.ds(bn, D)],
                                            1.0, None, ALU.mult))
                    settle()
                if kind != LAST:
                    add_unit(2 * j)
                if kind != LAST and j == 0:
                    moments_of(0, x_now, 2)
                if kind != LAST and j == 1:
                    dve.wait_ge(sd_ready, 1 if kind == FIRST else at(s, 2, 0))
                    normalise(0, x_now, x_n, xn_ready)
                if kind != FIRST and j == 5:
                    dve.wait_ge(sd_ready, at(s, 2, 1) if kind == MID else 2 * s)
                    normalise(1, x_mid, f_n, fn_ready)
                if adds_heads:
                    add_head(j, 0)
                elif with_small and j not in QUERY_SLOTS:
                    dve.wait_ge(small, small_count(kind, s, j))
                    if j in (2, 6, 20):
                        dve.tensor_copy((x_t if j == 2 else f_t)[:, :], ps_m[:, 0:128]).then_inc(small_out_v, 1)
                    else:
                        bp = snap(dve, ((s + (3 if j == 14 else 0)) % B) * D)
                        dve.tensor_tensor(x_all[:, :, :].rearrange("p b d -> p (b d)")[:, bass.ds(bp, D)],
                                          ps_m[:, 0:128], x_mid[:, :], ALU.add).then_inc(small_out_v, 1)
                if kind != LAST:
                    add_unit(2 * j + 1)
                if adds_heads:
                    add_head(j, 1)
                if j in (3, 19) and adds_heads:
                    dve.wait_ge(small_out_v, small_count(kind, s, j, "v"))
                    bp = snap(dve, ((s + (3 if j == 3 else 0)) % B) * D)
                    chain(dve.tensor_tensor(x_mid[:, :], x_all[:, :, :].rearrange("p b d -> p (b d)")[:, bass.ds(bp, D)],
                                            y_sum[:, :], ALU.add))
                    settle()
                    moments_of(1, x_mid, 3)
                    if j == 19:
                        dve.wait_ge(sd_ready, 2 * s + 1)
                        normalise(1, x_mid, f_n, fn_ready)
                if j % 2 == 0 and (kind != FIRST or j >= 1) and j <= NH:
                    dve.wait_ge(turned, at(s, 4 * NH, 4 * j))
                    dst = probs_t[:, ((j + 1) // 2 + 1) % 2, :].rearrange("p (k h f) -> p k h f", k=NB, h=2)
                    dve.tensor_copy(dst[:, 12:16, (j + 1) % 2, :],
                                    ps_t[:, 1, :].rearrange("p (k f) -> p k f", k=4)).then_inc(turned_out_v, 1)
                if with_small and j in QUERY_SLOTS:
                    group = QUERY_SLOTS.index(j)
                    heads = slice(4 * group, 4 * group + 4)
                    dve.wait_ge(upper_ready, at(s, 4, 1 + sorted(QUERY_SLOTS).index(j)))
                    dve.tensor_tensor(q_t[:, 1, heads, :], ps_m[:, :].rearrange("p (n f) -> p n f", n=4),
                                      q_t[:, 0, heads, :], ALU.subtract).then_inc(small_out_v, 1)
            return done[0]

        assert body(FIRST, 0) == TOTALS[0]
        with dve.Fori(1, STEPS - 1) as s:
            assert body(MID, s) == TOTALS[1]
        body(LAST, STEPS - 1)


def prologue(nc, a, mem, sem, sbuf, psum, v):
    x_all, ident, ones, half = v["x_all"], v["ident"], v["ones"], v["half"]
    stats, moments, dev, rdev = v["stats"], v["moments"], v["dev"], v["rdev"]
    ctx_t, side, ctx_n, q_t, w_score, w_value = (v[n] for n in ("ctx_t", "side", "ctx_n", "q_t", "w_score", "w_value"))
    bias, bias_sum, unit, mask, gw_all, gw_act, gw_dve, gw_pool = (
        v[n] for n in ("bias", "bias_sum", "unit", "mask", "gw_all", "gw_act", "gw_dve", "gw_pool"))
    x_t, x_n, x_now = v["x_t"], v["x_n"], v["x_now"]
    unit_ready, bias_added, mask_loaded, mask_ready = (v[n] for n in ("unit_ready", "bias_added", "mask_loaded", "mask_ready"))
    mask_summed = v["mask_summed"]
    score_dram, value_dram = v["score_dram"], v["value_dram"]
    weights = [a["L0_xattn_W" + n].rearrange("l d n h -> l d (n h)") for n in "qkv"]
    wo_dram = a["L0_xattn_Wo"].rearrange("l n h d -> l (n h) d").rearrange("l (c p) d -> l p c d", p=128)

    with ExitStack() as tmp:
        raw = sbuf(tmp, "raw", [128, 2, 4 * NH * HD])
        w_t = sbuf(tmp, "w_t", [128, 3, NH // 2, 128])
        ps = psum(tmp, "ps_pro", [128, 8, 512])

        filled = sem("filled")
        emptied_a, emptied_v = sem("emptied_a"), sem("emptied_v")
        x_in, gw_in = sem("x_in"), sem("gw_in")
        side_in = [sem(f"side_in{b}") for b in range(B)]
        raw_in = [sem(f"raw_in{i}") for i in range(2)]
        ctx_in = sem("ctx_in")
        merged_out = sem("score_weights_out"), sem("value_weights_out")
        consts, rows, powed, gw_own = sem("consts"), sem("rows"), sem("powed"), sem("gw_own")
        pro_gw_act = sem("pro_gw_act")
        uppers = sem("uppers")

        fills = []
        for i in range(L):
            fills += [("turn_w", i, w, c) for w in range(3) for c in range(2)]
            fills += [("turn_c", i, 0, c) for c in range(4)]
            fills += [("merge", i, w, c) for w in range(2) for c in range(4)]
        fills += [("turn_x", 0, 0, 0)] + [("query", 0, 0, c) for c in range(3)]
        where = {f: i for i, f in enumerate(fills)}

        split = [f[0] in ("turn_c", "query") for f in fills]
        by_vector = [split[i] or i % 2 == 1 for i in range(len(fills))]

        def emptied(eng, i):
            eng.wait_ge(emptied_v if by_vector[i] else emptied_a, by_vector[:i + 1].count(by_vector[i]))

        block = tmp.enter_context(nc.Block())

        @block.sync
        def _(sp):
            def store(i):
                for w, dst in enumerate((score_dram, value_dram)):
                    emptied(sp, where[("merge", i, w, 2)])
                    emptied(sp, where[("merge", i, w, 3)])
                    sp.dma_start(dst[L - 1 - i], (w_score, w_value)[w][:, :, :]).then_inc(merged_out[w], 16)

            sp.dma_start(x_all[:, :, :], v["x_dram"]).then_inc(x_in, 16)
            for l in range(L):
                gw = gw_all[:, l * 4 * K:(l + 1) * 4 * K]
                for n, name in enumerate(("Wth", "bth", "Wto")):
                    src = a["L0_xattn_" + name]
                    src = src[l:l + 1, :] if name == "bth" else src[l].rearrange("i k -> (i k)").rearrange("(o n) -> o n", o=1)
                    sp.dma_start(gw[:, n * K:(n + 1) * K], src.to_broadcast([128, K])).then_inc(gw_in, 16)
                sp.dma_start(gw[:, 3 * K:3 * K + 1], a["L0_xattn_bto"][l:l + 1, :].to_broadcast([128, 1])).then_inc(gw_in, 16)
            sp.dma_start(side[:, 0:T], v["side_dram"][0]).then_inc(side_in[0], 16)
            sp.dma_start(mask[:, :], v["mask_dram"][0:1, :].to_broadcast([128, T])).then_inc(mask_loaded, 16)
            for i in range(L):
                lay = L - 1 - i
                if i >= 2:
                    store(i - 2)
                    sp.wait_ge(filled, where[("merge", i - 2, 1, 3)] + 1)
                for w in range(3):
                    sp.dma_start(raw[:, i % 2, w * 1024:(w + 1) * 1024], weights[w][lay]).then_inc(raw_in[i % 2], 16)
                sp.dma_start(raw[:, i % 2, 3072:4096].rearrange("p (c d) -> p c d", d=128), wo_dram[lay]).then_inc(raw_in[i % 2], 16)
                if i >= 1:
                    sp.wait_ge(filled, where[("turn_c", i - 1, 0, 3)] + 1)
                sp.dma_start(ctx_n[:, :, :], v["ctx_dram"][B - 1 - i]).then_inc(ctx_in, 16)
                if i == 1:
                    sp.wait_ge(bias_added, 1)
                    sp.dma_start(mask[:, :], v["mask_dram"][1:2, :].to_broadcast([128, T])).then_inc(mask_loaded, 16)
                    for b in range(1, B):
                        sp.dma_start(side[:, b * T:(b + 1) * T], v["side_dram"][b]).then_inc(side_in[b], 16)
            for i in (2, 3):
                store(i)
            for w in range(2):
                sp.wait_ge(merged_out[w], 16 * L)
            for b in range(2, B):
                sp.wait_ge(side_in[b], 16)

        @block.gpsimd
        def _(pool):
            pool.memset(ident[:, :], 0.0).then_inc(consts, 1)
            pool.memset(ones[:, :], 1.0).then_inc(consts, 1)
            pool.memset(half[:, 0:1], 0.5).then_inc(consts, 1)
            pool.memset(half[:, 1:2], -0.5).then_inc(consts, 1)
            pool.memset(half[:, 2:3], Q_UP).then_inc(consts, 1)
            pool.wait_ge(consts, 5)
            pool.affine_select(out=ident[:, :], in_=ident[:, :], compare_op=ALU.not_equal, fill=1.0, base=0,
                               pattern=[[-1, 128]], channel_multiplier=1).then_inc(consts, 1)
            pool.wait_ge(gw_in, 16 * 4 * L)
            def add_bto(n):
                pool.wait_ge(mask_loaded, 16 * (n + 1))
                pool.tensor_tensor(mask[:, :], mask[:, :], gw_all[:, 3 * K:3 * K + 1].to_broadcast([128, T]),
                                   ALU.add).then_inc(mask_summed, 1)
                pool.wait_ge(mask_summed, n + 1)
                pool.tensor_tensor(mask[:, :], mask[:, :], half[:, 2:3].to_broadcast([128, T]),
                                   ALU.mult).then_inc(mask_ready, 1)

            add_bto(0)
            pool.wait_ge(rows, 1)
            pool.tensor_tensor(rdev[:, :], dev[:, :], half[:, 1:2].to_broadcast([128, B]), ALU.pow).then_inc(powed, 1)
            pool.wait_ge(rows, 2)
            pool.tensor_tensor(dev[:, 0:1], moments[:, 0, 1:2], half[:, 0:1], ALU.pow).then_inc(powed, 1)
            add_bto(1)

        @block.tensor
        def _(pe):
            pe.wait_ge(consts, 6)
            for n, (what, i, w, c) in enumerate(fills):
                if n >= 8:
                    emptied(pe, n - 8)
                bank = ps[:, n % 8, :]
                if what == "turn_w":
                    if (w, c) == (0, 0):
                        pe.wait_ge(raw_in[i % 2], 64 * (i // 2 + 1))
                    for k in range(4):
                        lo = w * 1024 + (4 * c + k) * 128
                        mm = pe.transpose(bank[:, k * 128:(k + 1) * 128], raw[:, i % 2, lo:lo + 128], ident[:, :])
                elif what == "turn_c":
                    if c == 0:
                        pe.wait_ge(ctx_in, 16 * (i + 1))
                    for k in range(4):
                        mm = pe.transpose(bank[:, k * 128:(k + 1) * 128], ctx_n[:, 4 * c + k, :], ident[:, :])
                elif what == "merge":
                    if (w, c) == (0, 0):
                        for k in range(6):
                            emptied(pe, where[("turn_w", i, k // 2, k % 2)])
                    odd, part = c // 2, c % 2
                    rows_ = slice(64 * odd, 64 * odd + 64)
                    for k in range(4):
                        pair = 4 * part + k
                        if w == 0:
                            lhs, rhs = w_t[rows_, 0, pair, :], w_t[rows_, 1, pair, :]
                        else:
                            lhs = w_t[rows_, 2, pair, :]
                            rhs = raw[rows_, i % 2, 3072 + pair * 128:3072 + (pair + 1) * 128]
                        mm = pe.matmul(bank[:, k * 128:(k + 1) * 128], lhs, rhs, start=True, stop=True)
                elif what == "turn_x":
                    pe.wait_ge(rows, 3)
                    mm = pe.transpose(bank[:, 0:128], x_n[:, :], ident[:, :])
                else:
                    if c == 0:
                        emptied(pe, where[("turn_x", 0, 0, 0)])
                        emptied(pe, where[("merge", L - 1, 1, 2)])
                        emptied(pe, where[("merge", L - 1, 1, 3)])
                    for k in range(4):
                        mm = pe.matmul(bank[:, k * 128:(k + 1) * 128], w_score[:, 4 * c + k, :], x_t[:, :],
                                       start=True, stop=True)
                mm.then_inc(filled, 1)

        def empty(eng, n, vector):
            what, i, w, c = fills[n]
            bank = ps[:, n % 8, :]
            eng.wait_ge(filled, n + 1)
            scale = 1.0
            if what == "turn_w":
                if i >= 1 and (w, c) in ((0, 0), (0, 1)):
                    eng.wait_ge(filled, where[("merge", i - 1, 1, 3)] + 1)
                if w == 0:
                    scale = float(HD) ** -0.5 * Q_UP
                dst, src = w_t[:, w, 4 * c:4 * c + 4, :], bank.rearrange("p (k f) -> p k f", k=4)
            elif what == "turn_c":
                lo = (B - 1 - i) * T + c * 512
                dst, src = ctx_t[:, int(vector), lo:lo + 512], bank
                upper = ctx_t[:, 0, lo:lo + 512]
            elif what == "merge":
                if i >= 1:
                    eng.wait_ge(merged_out[w], 16 * i)
                odd, part = c // 2, c % 2
                dst = (w_score, w_value)[w][:, :, :].rearrange("p (m two) d -> p m two d", two=2)[:, 4 * part:4 * part + 4, odd, :]
                src = bank.rearrange("p (k f) -> p k f", k=4)
            elif what == "turn_x":
                dst, src = x_t[:, :], bank[:, 0:128]
            else:
                dst, src = q_t[:, int(vector), 4 * c:4 * c + 4, :], bank.rearrange("p (k f) -> p k f", k=4)
                upper = q_t[:, 0, 4 * c:4 * c + 4, :]
            if split[n] and vector:
                eng.wait_ge(uppers, split[:n + 1].count(True))
                eng.tensor_tensor(dst, src, upper, ALU.subtract).then_inc(emptied_v, 1)
            elif split[n]:
                eng.activation(dst, src, ACT.Copy).then_inc(uppers, 1)
            elif vector:
                eng.tensor_scalar(dst, src, scale, None, ALU.mult).then_inc(emptied_v, 1)
            else:
                eng.activation(dst, src, ACT.Copy, scale=scale).then_inc(emptied_a, 1)

        mine = ([n for n in range(len(fills)) if split[n] or not by_vector[n]],
                [n for n in range(len(fills)) if by_vector[n]])

        @block.scalar
        def _(act):
            act.wait_ge(gw_in, 16 * 4 * L)
            act.activation(gw_act[:, :], gw_all[:, 0:2 * K], ACT.Copy).then_inc(pro_gw_act, 1)
            act.wait_ge(pro_gw_act, 1)
            act.wait_ge(side_in[0], 16)
            nf = 0
            for k in range(K + 1):
                if k >= 2:
                    act.wait_ge(bias_added, k - 1)
                if k == K:
                    act.wait_ge(side_in[1], 16)
                src = side[:, (k // K) * T:(k // K + 1) * T]
                act.activation(unit[:, k % 2, :], src, ACT.Relu, scale=gw_act[:, k % K:k % K + 1],
                               bias=gw_act[:, K + k % K:K + k % K + 1]).then_inc(unit_ready, 1)
                while nf < len(mine[0]) and nf * K < (k + 1) * len(mine[0]):
                    empty(act, mine[0][nf], False)
                    nf += 1

        @block.vector
        def _(dve):
            n_own = [0]

            def own(ins):
                ins.then_inc(gw_own, 1)
                n_own[0] += 1
                dve.wait_ge(gw_own, n_own[0])

            dve.wait_ge(x_in, 16)
            for b in range(B):
                own(dve.bn_stats(stats[:, b, :], x_all[:, b, :]))
                own(dve.bn_aggr(moments[:, b, :], stats[:, b, :]))
            dve.tensor_scalar(dev[:, :], moments[:, :, 1], LN_EPS, None, ALU.add).then_inc(rows, 1)
            dve.wait_ge(gw_in, 16 * 4 * L)
            wto = gw_all[:, :].rearrange("p (l n) -> p l n", l=L)[:, :, 2 * K:3 * K]
            own(dve.tensor_scalar(wto, wto, Q_UP, None, ALU.mult))
            own(dve.tensor_copy(gw_dve[:, :], gw_all[:, 2 * K:3 * K]))
            nf = 0
            for k in range(K):
                dve.wait_ge(unit_ready, k + 1)
                if k == 0:
                    dve.wait_ge(mask_ready, 1)
                else:
                    dve.wait_ge(bias_added, k)
                dve.scalar_tensor_tensor(out=(bias if k == K - 1 else bias_sum)[:, :], in0=unit[:, k % 2, :],
                                         scalar=gw_dve[:, k:k + 1], in1=(mask if k == 0 else bias_sum)[:, :],
                                         op0=ALU.mult, op1=ALU.add).then_inc(bias_added, 1)
                if k == 1:
                    dve.wait_ge(powed, 1)
                    for b in range(B):
                        own(dve.tensor_scalar(x_all[:, b, :], x_all[:, b, :], moments[:, b, 0:1], rdev[:, b:b + 1],
                                              ALU.subtract, ALU.mult))
                    own(dve.bn_stats(stats[:, 0, :], x_all[:, 0, :]))
                    dve.bn_aggr(moments[:, 0, :], stats[:, 0, :]).then_inc(rows, 1)
                if k == 4:
                    dve.wait_ge(powed, 2)
                    dve.wait_ge(rows, 2)
                    own(dve.tensor_scalar(dev[:, 0:1], dev[:, 0:1], NORM_EPS, None, ALU.add))
                    own(dve.reciprocal(rdev[:, 0:1], dev[:, 0:1]))
                    dve.tensor_scalar(x_n[:, :], x_all[:, 0, :], moments[:, 0, 0:1], rdev[:, 0:1],
                                      ALU.subtract, ALU.mult).then_inc(rows, 1)
                while nf < len(mine[1]) and nf * K < (k + 1) * len(mine[1]):
                    empty(dve, mine[1][nf], True)
                    nf += 1


def self_attention_and_experts(nc, a, out, top, mem, sem, sbuf, psum, v):
    x_all, ident, ones, half = v["x_all"], v["ident"], v["ones"], v["half"]
    stats, moments, dev, rdev = v["stats"], v["moments"], v["dev"], v["rdev"]
    x_in0 = sbuf(mem, "x_in0", [128, B, D])
    w_q = sbuf(mem, "w_q", [128, 4, 4, 32])
    w_k = sbuf(mem, "w_k", [128, 4, 4, 32])
    w_v = sbuf(mem, "w_v", [128, SH, SK])
    w_o = sbuf(mem, "w_o", [128, 128])
    b_q = sbuf(mem, "b_q", [128, 4])
    b_k = sbuf(mem, "b_k", [128, 4])
    b_q_rows = sbuf(mem, "b_q_rows", [4, 4, 32])
    b_k_rows = sbuf(mem, "b_k_rows", [4, 4, 32])
    b_v = sbuf(mem, "b_v", [1, 128])
    b_o = sbuf(mem, "b_o", [1, 128])
    causal = sbuf(mem, "causal", [128, 128])
    gate = sbuf(mem, "gate", [NE, D])
    gate_t = sbuf(mem, "gate_t", [128, NE])
    w1 = sbuf(mem, "w1", [128, NE, FILT])
    w2 = sbuf(mem, "w2", [128, NE * FC, D])
    b1 = sbuf(mem, "b1", [NE * FC, 128])
    b1_t = sbuf(mem, "b1_t", [128, NE * FC])
    b2 = sbuf(mem, "b2", [1, NE * D])
    index = sbuf(mem, "index", [128, B, NE])
    xn = sbuf(mem, "xn", [128, B, D])
    xn_t = sbuf(mem, "xn_t", [128, B * F])
    qh = sbuf(mem, "qh", [128, 4, B * F])
    kh = sbuf(mem, "kh", [128, 4, B * F])
    vh = sbuf(mem, "vh", [128, B, 128])
    att = sbuf(mem, "att", [128, 2, SH, F])
    att_t = sbuf(mem, "att_t", [128, SH, F])
    peak = sbuf(mem, "peak", [128, SH])
    total = sbuf(mem, "total", [128, 2, SH])
    mixed = sbuf(mem, "mixed", [128, SH, SK])
    mixed_t = sbuf(mem, "mixed_t", [128, 128])
    hid = sbuf(mem, "hid", [128, 2, FC, B * F])
    y = sbuf(mem, "y", [128, B, D])
    g = {n: sbuf(mem, "gate_" + n, [128, B, NE]) for n in ("z", "p", "m", "c", "one", "two", "left", "w")}
    g1 = {n: sbuf(mem, "gcol_" + n, [128, B]) for n in ("top", "sum", "best", "pick", "second", "pick2")}

    ps_a = psum(mem, "ps_a", [128, 4, 512])
    ps_b = psum(mem, "ps_b", [128, 4, 512])

    x_in, att_in, moe_in = sem("x0_in"), sem("att_in"), sem("moe_in")
    zeroed, masked = sem("zeroed"), sem("masked")
    ve_step, dev_in, powed2 = sem("ve_step"), sem("dev_in"), sem("powed2")
    first_norm, rows_n = sem("first_norm"), sem("rows_n")
    pa, pa_out_a, pa_out_v = sem("pa"), sem("pa_out_a"), sem("pa_out_v")
    s_ready, s_shift, s_exp, t_ready, t_out = sem("s_ready"), sem("s_shift"), sem("s_exp"), sem("t_ready"), sem("t_out")
    s_taken = sem("s_taken")
    c_ready, c_out, ct_ready, ct_out, o_ready, o_out = (sem(n) for n in ("c_ready", "c_out", "ct_ready", "ct_out", "o_ready", "o_out"))
    x_t2, x_t2_out, gl_ready, gl_out, gexp = (sem(n) for n in ("x_t2", "x_t2_out", "gl_ready", "gl_out", "gexp"))
    h_ready, h_out, y_ready, y_out, stored = (sem(n) for n in ("h_ready", "h_out", "y_ready", "y_out", "stored"))
    gshift, bt_ready, bt_out = sem("gshift"), sem("bt_ready"), sem("bt_out")

    block = mem.enter_context(nc.Block())

    @block.sync
    def _(sp):
        sp.dma_start(x_in0[:, :, :], v["x_dram"]).then_inc(x_in, 16)
        sp.dma_start(gate[:, :], a["L0_ffn_gate_w"]).then_inc(att_in, 16)
        sp.dma_start(b1[:, :], a["L0_ffn_b1"].rearrange("e (c p) -> (e c) p", p=128)).then_inc(att_in, 16)
        sp.dma_start(w_v[:, :, :], a["L0_attn_Wv"].rearrange("h d k -> d h k")).then_inc(att_in, 16)
        sp.dma_start(w_o[:, :], a["L0_attn_Wo"]).then_inc(att_in, 16)
        sp.dma_start(b_v[:, :], a["L0_attn_bv"].rearrange("(o h) k -> o (h k)", o=1)).then_inc(att_in, 16)
        sp.dma_start(b_o[:, :], a["L0_attn_bo"].rearrange("(o n) -> o n", o=1)).then_inc(att_in, 16)
        sp.wait_ge(zeroed, 4)
        for w, b, n in ((w_q, b_q_rows, "q"), (w_k, b_k_rows, "k")):
            for c in range(4):
                sp.dma_start(w[:, c, :, 0:SK], a["L0_attn_W" + n][4 * c:4 * c + 4].rearrange("h d k -> d h k")).then_inc(att_in, 16)
            sp.dma_start(b[:, :, 0:SK], a["L0_attn_b" + n].rearrange("(c j) k -> c j k", j=4)).then_inc(att_in, 16)
        for e in range(NE):
            sp.dma_start(w1[:, e, :], a["L0_ffn_w1"][e]).then_inc(moe_in, 16)
            sp.dma_start(w2[:, e * FC:(e + 1) * FC, :], a["L0_ffn_w2"][e].rearrange("(c p) d -> p c d", p=128)).then_inc(moe_in, 16)
        sp.dma_start(b2[:, :], a["L0_ffn_b2"].rearrange("(o e) d -> o (e d)", o=1)).then_inc(moe_in, 16)
        sp.wait_ge(y_out, NE)
        sp.dma_start(out.rearrange("b f d -> f b d"), y[:, :, :]).then_inc(stored, 16)
        sp.wait_ge(stored, 16)

    ATT_IN = 16 * (6 + 2 * 5)

    @block.gpsimd
    def _(pool):
        for t in (w_q, w_k):
            pool.memset(t[:, :, :, :], 0.0).then_inc(zeroed, 1)
        for t in (b_q_rows, b_k_rows):
            pool.memset(t[:, :, :], 0.0).then_inc(zeroed, 1)
        pool.memset(causal[:, :], 0.0).then_inc(masked, 1)
        pool.wait_ge(masked, 1)
        pool.affine_select(out=causal[:, :], in_=causal[:, :], compare_op=ALU.is_ge, fill=NEG, base=0,
                           pattern=[[-1, 128]], channel_multiplier=1).then_inc(masked, 1)
        for e in range(NE):
            pool.memset(index[:, :, e], float(e)).then_inc(masked, 1)
        for n in range(3):
            pool.wait_ge(dev_in, n + 1)
            pool.tensor_tensor(rdev[:, :], dev[:, :], half[:, (n > 0):(n > 0) + 1].to_broadcast([128, B]),
                               ALU.pow).then_inc(powed2, 1)

    @block.tensor
    def _(pe):
        pe.wait_ge(att_in, ATT_IN)
        pe.transpose(ps_b[:, 0, 0:NE], gate[:, :], ident[0:NE, 0:NE])
        for i, t in enumerate((b_q_rows, b_k_rows)):
            pe.transpose(ps_b[:, 2, 4 * i:4 * i + 4], t[:, :, :].rearrange("c j k -> c (j k)"), ident[0:4, 0:4])
        pe.transpose(ps_b[:, 1, 0:NE * FC], b1[:, :], ident[0:NE * FC, 0:NE * FC]).then_inc(bt_ready, 1)
        pe.wait_ge(rows_n, B)
        for b in range(B):
            mm = pe.transpose(ps_a[:, 0, b * 128:(b + 1) * 128], xn[:, b, :], ident[:, :])
        mm.then_inc(pa, 1)
        pe.wait_ge(pa_out_v, 1)
        n = 0
        for w in (w_q, w_k):
            for c in range(4):
                bank = 1 + n % 3
                if n >= 3:
                    pe.wait_ge(pa_out_a, n - 2)
                pe.matmul(ps_a[:, bank, :], w[:, c, :, :].rearrange("p j k -> p (j k)"), xn_t[:, :],
                          start=True, stop=True).then_inc(pa, 1)
                n += 1
        pe.wait_ge(bt_out, 4)
        for b in range(B):
            o = ps_a[:, 0, b * 128:(b + 1) * 128]
            pe.matmul(o, xn_t[:, b * 128:(b + 1) * 128], w_v[:, :, :].rearrange("p h k -> p (h k)"),
                      start=b == 0, stop=False, skip_group_check=True)
            mm = pe.matmul(o, ones[0:1, :], b_v[0:1, :], start=False, stop=True, skip_group_check=True)
        mm.then_inc(pa, 1)
        pe.wait_ge(pa_out_a, 8)
        pe.wait_ge(pa_out_v, 2)

        def logits(b):
            if b >= 1:
                pe.wait_ge(s_taken, b)
            for c in range(4):
                for j in range(4):
                    r = slice(32 * j, 32 * j + 32)
                    mm = pe.matmul(ps_a[:, j, c * 128:(c + 1) * 128], qh[r, c, b * 128:(b + 1) * 128],
                                   kh[r, c, b * 128:(b + 1) * 128], start=True, stop=True)
            mm.then_inc(s_ready, 1)

        logits(0)
        for b in range(B):
            if b + 1 < B:
                logits(b + 1)
            pe.wait_ge(s_exp, b + 1)
            if b >= 1:
                pe.wait_ge(o_out, b)
            for h in range(SH):
                mm = pe.transpose(ps_b[:, h // 4, (h % 4) * 128:(h % 4 + 1) * 128], att[:, b % 2, h, :], ident[:, :])
            mm.then_inc(t_ready, 1)
            pe.wait_ge(t_out, b + 1)
            for h in range(SH):
                real = 4 * (h % 4) + h // 4
                mm = pe.matmul(ps_b[:, 0, real * SK:(real + 1) * SK], att_t[:, h, :], vh[:, b, real * SK:(real + 1) * SK],
                               start=True, stop=True)
            mm.then_inc(c_ready, 1)
            pe.wait_ge(c_out, b + 1)
            pe.transpose(ps_b[:, 1, 0:128], mixed[:, :, :].rearrange("p h k -> p (h k)"), ident[:, :]).then_inc(ct_ready, 1)
            pe.wait_ge(ct_out, b + 1)
            pe.matmul(ps_b[:, 2, 0:128], mixed_t[:, :], w_o[:, :], start=True, stop=False)
            pe.matmul(ps_b[:, 2, 0:128], ones[0:1, :], b_o[0:1, :], start=False, stop=True).then_inc(o_ready, 1)

        pe.wait_ge(rows_n, 2 * B)
        for b in range(B):
            mm = pe.transpose(ps_a[:, 0, b * 128:(b + 1) * 128], xn[:, b, :], ident[:, :])
        mm.then_inc(x_t2, 1)
        pe.wait_ge(x_t2_out, 1)
        for b in range(B):
            mm = pe.matmul(ps_b[:, 3, b * NE:(b + 1) * NE], xn_t[:, b * 128:(b + 1) * 128], gate_t[:, :],
                           start=True, stop=True)
        mm.then_inc(gl_ready, 1)
        pe.wait_ge(moe_in, 16 * (2 * NE + 1))

        def hidden(e):
            for c in range(FC):
                n = e * FC + c
                if n >= FC:
                    pe.wait_ge(h_out, n - FC + 1)
                pe.matmul(ps_a[:, c, :], w1[:, e, c * 128:(c + 1) * 128], xn_t[:, :],
                          start=True, stop=True).then_inc(h_ready, 1)

        hidden(0)
        for e in range(NE):
            if e + 1 < NE:
                hidden(e + 1)
            pe.wait_ge(h_out, FC * (e + 1))
            if e >= 2:
                pe.wait_ge(y_out, e - 1)
            for b in range(B):
                o = ps_b[:, e % 2, b * 128:(b + 1) * 128]
                for c in range(FC):
                    pe.matmul(o, hid[:, e % 2, c, b * 128:(b + 1) * 128], w2[:, e * FC + c, :],
                              start=b == 0 and c == 0, stop=False, skip_group_check=True)
                mm = pe.matmul(o, ones[0:1, :], b2[0:1, e * D:(e + 1) * D], start=False, stop=True, skip_group_check=True)
            mm.then_inc(y_ready, 1)

    @block.scalar
    def _(act):
        n = 0
        act.wait_ge(bt_out, 4)
        for w in range(2):
            for c in range(4):
                act.wait_ge(pa, n + 2)
                act.activation((qh, kh)[w][:, c, :], ps_a[:, 1 + n % 3, :], ACT.Identity,
                               bias=(b_q, b_k)[w][:, c:c + 1]).then_inc(pa_out_a, 1)
                n += 1
        for b in range(B):
            act.wait_ge(s_shift, b + 1)
            act.activation(att[:, b % 2, :, :], att[:, b % 2, :, :], ACT.Exp).then_inc(s_exp, 1)
            act.wait_ge(t_ready, b + 1)
            act.activation(att_t[:, :, :].rearrange("p (a b) f -> p a (b f)", a=4), ps_b[:, :, :], ACT.Copy).then_inc(t_out, 1)
        act.wait_ge(gshift, 1)
        act.activation(g["p"][:, :, :], g["z"][:, :, :], ACT.Exp).then_inc(gexp, 1)
        for e in range(NE):
            for c in range(FC):
                n = e * FC + c
                act.wait_ge(h_ready, n + 1)
                if e >= 2:
                    act.wait_ge(y_ready, e - 1)
                act.activation(hid[:, e % 2, c, :], ps_a[:, c, :], ACT.Silu, bias=b1_t[:, n:n + 1]).then_inc(h_out, 1)

    @block.vector
    def _(dve):
        n_own = [0]

        def own(ins):
            ins.then_inc(ve_step, 1)
            n_own[0] += 1
            dve.wait_ge(ve_step, n_own[0])

        def row_moments():
            for b in range(B):
                own(dve.bn_stats(stats[:, b, :], x_all[:, b, :]))
                own(dve.bn_aggr(moments[:, b, :], stats[:, b, :]))

        def normalise(ready):
            for b in range(B):
                dve.tensor_scalar(xn[:, b, :], x_all[:, b, :], moments[:, b, 0:1], rdev[:, b:b + 1],
                                  ALU.subtract, ALU.mult).then_inc(ready, 1)

        row_moments()
        dve.tensor_copy(dev[:, :], moments[:, :, 1]).then_inc(dev_in, 1)
        dve.wait_ge(powed2, 1)
        own(dve.tensor_scalar(rdev[:, :], rdev[:, :], NORM_EPS, None, ALU.add))
        own(dve.reciprocal(rdev[:, :], rdev[:, :]))
        normalise(first_norm)
        dve.wait_ge(first_norm, B)
        dve.wait_ge(x_in, 16)
        own(dve.tensor_tensor(x_all[:, :, :], xn[:, :, :], x_in0[:, :, :], ALU.add))
        row_moments()
        dve.tensor_scalar(dev[:, :], moments[:, :, 1], LN_EPS, None, ALU.add).then_inc(dev_in, 1)
        dve.wait_ge(powed2, 2)
        normalise(rows_n)
        dve.wait_ge(bt_ready, 1)
        dve.tensor_copy(gate_t[:, :], ps_b[:, 0, 0:NE]).then_inc(bt_out, 1)
        dve.tensor_copy(b1_t[:, :], ps_b[:, 1, 0:NE * FC]).then_inc(bt_out, 1)
        dve.tensor_copy(b_q[:, :], ps_b[:, 2, 0:4]).then_inc(bt_out, 1)
        dve.tensor_copy(b_k[:, :], ps_b[:, 2, 4:8]).then_inc(bt_out, 1)
        dve.wait_ge(pa, 1)
        dve.tensor_copy(xn_t[:, :], ps_a[:, 0, :]).then_inc(pa_out_v, 1)
        dve.wait_ge(pa, 10)
        dve.tensor_copy(vh[:, :, :].rearrange("p b n -> p (b n)"), ps_a[:, 0, :]).then_inc(pa_out_v, 1)
        dve.wait_ge(masked, 2 + NE)

        def shifted(b):
            dve.wait_ge(s_ready, b + 1)
            if b >= 2:
                dve.wait_ge(t_ready, b - 1)
            lg = att[:, b % 2, :, :]
            dve.scalar_tensor_tensor(out=lg, in0=ps_a[:, :, :].rearrange("p a (c f) -> p (a c) f", c=4),
                                     scalar=float(SK) ** -0.5,
                                     in1=causal[:, :].unsqueeze(1).to_broadcast([128, SH, F]),
                                     op0=ALU.mult, op1=ALU.add).then_inc(s_taken, 1)
            dve.wait_ge(s_taken, b + 1)
            own(dve.tensor_reduce(peak[:, :], lg, AX.X, ALU.max))
            dve.tensor_tensor(lg, lg, peak[:, :].unsqueeze(2).to_broadcast([128, SH, F]), ALU.subtract).then_inc(s_shift, 1)

        shifted(0)
        for b in range(B):
            if b + 1 < B:
                shifted(b + 1)
            dve.wait_ge(s_exp, b + 1)
            own(dve.tensor_reduce(total[:, 0, :], att[:, b % 2, :, :], AX.X, ALU.add))
            own(dve.reciprocal(total[:, 1, :].rearrange("p (c j) -> p j c", c=4),
                               total[:, 0, :].rearrange("p (j c) -> p j c", j=4)))
            dve.wait_ge(c_ready, b + 1)
            dve.tensor_tensor(mixed[:, :, :], ps_b[:, 0, 0:128].rearrange("p (h k) -> p h k", k=SK),
                              total[:, 1, :].unsqueeze(2).to_broadcast([128, SH, SK]), ALU.mult).then_inc(c_out, 1)
            dve.wait_ge(ct_ready, b + 1)
            dve.tensor_copy(mixed_t[:, :], ps_b[:, 1, 0:128]).then_inc(ct_out, 1)
            dve.wait_ge(o_ready, b + 1)
            dve.tensor_tensor(x_all[:, b, :], ps_b[:, 2, 0:128], x_all[:, b, :], ALU.add).then_inc(o_out, 1)
        dve.wait_ge(o_out, B)
        row_moments()
        dve.tensor_scalar(dev[:, :], moments[:, :, 1], LN_EPS, None, ALU.add).then_inc(dev_in, 1)
        dve.wait_ge(powed2, 3)
        normalise(rows_n)
        dve.wait_ge(x_t2, 1)
        dve.tensor_copy(xn_t[:, :], ps_a[:, 0, :]).then_inc(x_t2_out, 1)

        def col(n):
            return g1[n][:, :].unsqueeze(2).to_broadcast([128, B, NE])

        dve.wait_ge(gl_ready, 1)
        own(dve.tensor_copy(g["z"][:, :, :], ps_b[:, 3, 0:B * NE].rearrange("p (b e) -> p b e", b=B)))
        own(dve.tensor_reduce(g1["top"][:, :], g["z"][:, :, :], AX.X, ALU.max))
        dve.tensor_tensor(g["z"][:, :, :], g["z"][:, :, :], col("top"), ALU.subtract).then_inc(gshift, 1)
        dve.wait_ge(gexp, 1)
        own(dve.tensor_reduce(g1["sum"][:, :], g["p"][:, :, :], AX.X, ALU.add))
        own(dve.reciprocal(g1["sum"][:, :], g1["sum"][:, :]))
        own(dve.tensor_tensor(g["left"][:, :, :], g["p"][:, :, :], col("sum"), ALU.mult))
        own(dve.tensor_copy(g["p"][:, :, :], g["left"][:, :, :]))
        for pick in ("one", "two"):
            own(dve.tensor_reduce(g1["best"][:, :], g["left"][:, :, :], AX.X, ALU.max))
            own(dve.tensor_tensor(g["m"][:, :, :], g["left"][:, :, :], col("best"), ALU.is_lt))
            own(dve.scalar_tensor_tensor(out=g["c"][:, :, :], in0=g["m"][:, :, :], scalar=float(NE),
                                         in1=index[:, :, :], op0=ALU.mult, op1=ALU.add))
            own(dve.tensor_reduce(g1["pick"][:, :], g["c"][:, :, :], AX.X, ALU.min))
            own(dve.tensor_tensor(g[pick][:, :, :], index[:, :, :], col("pick"), ALU.is_equal))
            if pick == "one":
                own(dve.scalar_tensor_tensor(out=g["left"][:, :, :], in0=g["one"][:, :, :], scalar=-2.0,
                                             in1=g["left"][:, :, :], op0=ALU.mult, op1=ALU.add))
        own(dve.tensor_tensor(g["one"][:, :, :], g["one"][:, :, :], g["two"][:, :, :], ALU.add))
        own(dve.tensor_tensor(g["w"][:, :, :], g["one"][:, :, :], g["p"][:, :, :], ALU.mult))

        for e in range(NE):
            dve.wait_ge(y_ready, e + 1)
            if e:
                dve.wait_ge(y_out, e)
            for b in range(B):
                ins = dve.scalar_tensor_tensor(out=y[:, b, :], in0=ps_b[:, e % 2, b * 128:(b + 1) * 128],
                                               scalar=g["w"][:, b, e:e + 1], in1=(y if e else x_all)[:, b, :],
                                               op0=ALU.mult, op1=ALU.add)
            ins.then_inc(y_out, 1)


_INS = ["x", "ctx_1024", "fside_BxSxS2_0", "mask_Bx1x1xS2_ff0"] + \
    ["L0_xattn_" + n for n in ("Wq", "Wk", "Wv", "Wo", "Wth", "bth", "Wto", "bto", "Wf1", "bf1", "Wf2", "bf2")] + \
    ["L0_attn_" + n for n in ("Wq", "bq", "Wk", "bk", "Wv", "bv", "Wo", "bo")] + \
    ["L0_ffn_" + n for n in ("gate_w", "w1", "b1", "w2", "b2")]


def kernel(**inputs):
    import numpy as np
    import concourse.bacc as bacc
    from concourse.bass_utils import run_bass_kernel_spmd

    nc = bacc.Bacc("TRN2", target_bir_lowering=False, num_devices=1)
    arrays, aps = {}, {}
    for name in _INS:
        array = np.ascontiguousarray(inputs[name])
        arrays["in_" + name] = array
        aps[name] = nc.dram_tensor("in_" + name, array.shape, mybir.dt.from_np(array.dtype), kind="ExternalInput").ap()
    out = nc.dram_tensor("out", (B, F, D), F32, kind="ExternalOutput").ap()
    perceiver(nc, aps, out)
    result = run_bass_kernel_spmd(nc, [arrays], core_ids=[0])
    return result.results[0]["out"]
```

```python
from contextlib import ExitStack

import concourse.bass as bass
from concourse import mybir

F32 = mybir.dt.float32
F16 = mybir.dt.float16
ALU = mybir.AluOpType
ACT = mybir.ActivationFunctionType
AX = mybir.AxisListType

B, F, D = 4, 128, 128
T = 2048
L, NH, HD = 4, 16, 64
K = 32
FILT = 512
NB = T // 128
FC = FILT // 128
STEPS = L * B
NORM_EPS = 1e-6
Q_UP = 64.0
LN_EPS = 1e-5
NE = 8
SH, SK = 16, 8
NEG = -1.0e9
LOW = -3.0e38

FIRST, MID, LAST = 0, 1, 2

SMALL = {
    FIRST: {0: "v", 2: "v", 4: "v", 5: "v", 7: "v", 8: "v", 9: "v", 11: "v", 12: "v", 13: "v", 15: "v"},
    MID: {0: "v", 1: "v", 2: "v", 3: "v", 4: "v", 5: "v", 6: "v", 7: "v", 8: "v", 9: "v", 10: "a",
          11: "v", 12: "v", 13: "v", 14: "v", 15: "v"},
    LAST: {0: "v", 1: "v", 3: "v", 5: "v", 6: "v", 7: "v", 9: "v", 10: "a", 11: "v", 13: "v", 14: "v",
           15: "v", 17: "v", 19: "v", 20: "v", 21: "a", 22: "v"},
}
QUERY_SLOTS = (4, 8, 12, 0)
LAST_SLOTS = 23


def snap(eng, value):
    return value if isinstance(value, int) else eng.snap(value)


def small_count(kind, s, slot, who="av"):
    def n(k, upto=99):
        return sum(1 for j, w in SMALL[k].items() if w in who and j <= upto)
    if kind == FIRST:
        return n(FIRST, slot)
    if kind == MID:
        return (s - 1) * n(MID) + (n(FIRST) + n(MID, slot))
    return n(FIRST) + (STEPS - 2) * n(MID) + n(LAST, slot)


def by_engine(kind, s, slot):
    own = [j for j in SMALL[kind] if j < slot]
    if own:
        j = max(own)
        return SMALL[kind][j], small_count(kind, s, j, SMALL[kind][j])
    if kind == FIRST:
        return None, 0
    w = SMALL[MID][15]
    return w, small_count(kind, s, -1, w)


CHUNKS_A, CHUNKS_V = 3 * NH + NH // 2, NH // 2


def chunks_a(s, slot, c):
    assert c < 3 or slot % 2 == 1
    return s * CHUNKS_A + (3 * (slot - 1) + slot // 2 + c + 1)


def chunks_v(s, slot):
    assert slot % 2 == 0
    return s * CHUNKS_V + slot // 2


def perceiver(nc, a, out):
    xq, xk, xv, xo = (a["L0_xattn_" + n] for n in ("Wq", "Wk", "Wv", "Wo"))
    score_dram = nc.dram_tensor("score_weights", (L, 128, NH, 128), F32, kind="Internal").ap()
    value_dram = nc.dram_tensor("value_weights", (L, 128, NH, 128), F32, kind="Internal").ap()
    x_dram = a["x"].rearrange("b f d -> f b d")
    ctx_dram = a["ctx_1024"].rearrange("b (k p) d -> b p k d", p=128)
    side_dram = a["fside_BxSxS2_0"]
    mask_dram = a["mask_Bx1x1xS2_ff0"].rearrange("b o n t -> (b o n) t")

    with ExitStack() as top:
        def sem(name):
            return top.enter_context(nc.semaphore(name))

        def sbuf(ctx, name, shape, dtype=F32):
            return ctx.enter_context(nc.sbuf_tensor(name, shape, dtype))

        def psum(ctx, name, shape):
            return ctx.enter_context(nc.psum_tensor(name, shape, F32))

        x_all = sbuf(top, "x_all", [128, B, D])
        ident = sbuf(top, "ident", [128, 128])
        ones = sbuf(top, "ones", [128, 128])
        half = sbuf(top, "half", [128, 3])
        stats = sbuf(top, "stats", [128, B, 6])
        moments = sbuf(top, "moments", [128, B, 2])
        dev = sbuf(top, "dev", [128, B])
        rdev = sbuf(top, "rdev", [128, B])

        with ExitStack() as mem:
            cross_attention(nc, a, top, mem, sem, sbuf, psum, locals())
        with ExitStack() as mem:
            self_attention_and_experts(nc, a, out, top, mem, sem, sbuf, psum, locals())


def cross_attention(nc, a, top, mem, sem, sbuf, psum, g_):
    x_all, ident, ones, half = g_["x_all"], g_["ident"], g_["ones"], g_["half"]
    stats, moments, dev, rdev = g_["stats"], g_["moments"], g_["dev"], g_["rdev"]
    score_dram, value_dram, x_dram = g_["score_dram"], g_["value_dram"], g_["x_dram"]
    ctx_dram, side_dram, mask_dram = g_["ctx_dram"], g_["side_dram"], g_["mask_dram"]

    ctx_t = sbuf(mem, "ctx_t", [128, 2, B * T], F16)
    side = sbuf(mem, "side", [128, B * T])
    ctx_n = sbuf(mem, "ctx_n", [128, NB, 128])
    q_t = sbuf(mem, "q_t", [128, 2, NH, 128], F16)
    w_score = sbuf(mem, "w_score", [128, NH, 128])
    w_value = sbuf(mem, "w_value", [128, NH, 128])
    bias = sbuf(mem, "bias", [128, T])
    bias_sum = sbuf(mem, "bias_sum", [128, T])
    unit = sbuf(mem, "unit", [128, 2, T])
    mask = sbuf(mem, "mask", [128, T])
    gw_all = sbuf(mem, "gw_all", [128, L * 4 * K])
    gw_act = sbuf(mem, "gw_act", [128, 2 * K])
    gw_dve = sbuf(mem, "gw_dve", [128, K])
    gw_pool = sbuf(mem, "gw_pool", [128, 1])
    bf1_t = sbuf(mem, "bf1_t", [128, L * FC])
    bf1_now = sbuf(mem, "bf1_now", [128, FC])
    x_t = sbuf(mem, "x_t", [128, 128])
    x_n = sbuf(mem, "x_n", [128, 128])
    x_now = sbuf(mem, "x_now", [128, 128])

    unit_ready, bias_added = sem("unit_ready"), sem("bias_added")
    mask_loaded, mask_summed, mask_ready = sem("mask_loaded"), sem("mask_summed"), sem("mask_ready")

    prologue(nc, a, mem, sem, sbuf, psum, {**g_, **locals()})

    probs = sbuf(mem, "probs", [128, 2, T])
    probs_t = sbuf(mem, "probs_t", [128, 2, NB * 256])
    mix_t = sbuf(mem, "mix_t", [128, 256])
    y_sum = sbuf(mem, "y_sum", [128, 128])
    x_mid = sbuf(mem, "x_mid", [128, 128])
    f_n = sbuf(mem, "f_n", [128, 128])
    f_t = sbuf(mem, "f_t", [128, 128])
    hid_t = sbuf(mem, "hid_t", [128, FILT])
    wf1 = sbuf(mem, "wf1", [128, FILT])
    wf2 = sbuf(mem, "wf2", [128, FC, 128])
    bf2 = sbuf(mem, "bf2", [1, 128])
    tops = sbuf(mem, "tops", [128, 2])
    negmax = sbuf(mem, "negmax", [128, 2])
    sums = sbuf(mem, "sums", [128, NH])
    rsum = sbuf(mem, "rsum", [128, 2])
    mom = sbuf(mem, "mom", [128, 2, 2])
    st = sbuf(mem, "st", [128, 2, 6])
    sd = sbuf(mem, "sd", [128, 2])
    rs = sbuf(mem, "rs", [128, 2])
    pace = sbuf(mem, "pace", [128, 4])

    ps_s = psum(mem, "ps_s", [128, T])
    ps_t = psum(mem, "ps_t", [128, 2, 512])
    ps_u = psum(mem, "ps_u", [128, 512])
    ps_m = psum(mem, "ps_m", [128, 512])

    scored = sem("scored")
    taken = sem("taken")
    max_ready = sem("max_ready")
    exp_ready = sem("exp_ready")
    turned = sem("turned")
    turned_out_a = sem("turned_out_a")
    turned_out_v = sem("turned_out_v")
    mixing = sem("mixing")
    mix_out = sem("mix_out")
    small = sem("small")
    small_out_a, small_out_v = sem("small_out_a"), sem("small_out_v")
    upper_ready = sem("upper_ready")
    y_added = sem("y_added")
    xn_ready = sem("xn_ready")
    fn_ready = sem("fn_ready")
    mom_ready = sem("mom_ready")
    sd_ready = sem("sd_ready")
    bto_here = sem("bto_here")
    dve_step = sem("dve_step")
    gw_act_ready = sem("gw_act_ready")
    bf1_ready = sem("bf1_ready")
    w_score_in, w_value_in = sem("w_score_in"), sem("w_value_in")
    ctx_lo_in, ctx_hi_in, ffn_in = sem("ctx_lo_in"), sem("ctx_hi_in"), sem("ffn_in")

    def at(s, per, off):
        return s * per + off

    def steps(eng, body):
        body(FIRST, 0)
        with eng.Fori(1, STEPS - 1) as s:
            body(MID, s)
        body(LAST, STEPS - 1)

    def slots(kind):
        return range(LAST_SLOTS if kind == LAST else NH)

    block = mem.enter_context(nc.Block())

    @block.sync
    def _(sp):
        def body(kind, s):
            if kind != FIRST:
                sp.wait_ge(small, small_count(kind, s, -1))
                lay = snap(sp, (s - 1) // B)
                sp.dma_start(wf1[:, :], a["L0_xattn_Wf1"][bass.ds(lay, 1), :, :].rearrange("l d n -> d (l n)")).then_inc(ffn_in, 16)
                sp.dma_start(wf2[:, :, :], a["L0_xattn_Wf2"][bass.ds(lay, 1), :, :].rearrange("l (c p) d -> p (l c) d", p=128)).then_inc(ffn_in, 16)
                sp.dma_start(bf2[:, :], a["L0_xattn_bf2"][bass.ds(lay, 1), :]).then_inc(ffn_in, 16)
            if kind == MID:
                sp.wait_ge(small, small_count(kind, s, 0))
                lay = snap(sp, (s + 1) // B)
                sp.dma_start(w_score[:, :, :], score_dram[bass.ds(lay, 1)].rearrange("l p n d -> p (l n) d")).then_inc(w_score_in, 16)
            if kind != LAST:
                sp.wait_ge(bias_added, at(s, K, K + 1))
                b2 = snap(sp, (s + 2) % B)
                sp.dma_start(mask[:, :], mask_dram[bass.ds(b2, 1), :].to_broadcast([128, T])).then_inc(mask_loaded, 16)
            if kind != FIRST:
                b0 = snap(sp, s % B)
                sp.wait_ge(mixing, at(s, NH, -1))
                sp.dma_start(ctx_n[:, 0:NB // 2, :], ctx_dram[bass.ds(b0, 1), :, 0:NB // 2, :].rearrange("b p k d -> p (b k) d")).then_inc(ctx_lo_in, 16)
                sp.wait_ge(mixing, at(s, NH, 0))
                sp.dma_start(ctx_n[:, NB // 2:NB, :], ctx_dram[bass.ds(b0, 1), :, NB // 2:NB, :].rearrange("b p k d -> p (b k) d")).then_inc(ctx_hi_in, 16)
                sp.wait_ge(small, small_count(kind, s, 3))
                lay = snap(sp, s // B)
                sp.dma_start(w_value[:, :, :], value_dram[bass.ds(lay, 1)].rearrange("l p n d -> p (l n) d")).then_inc(w_value_in, 16)

        steps(sp, body)

    @block.gpsimd
    def _(pool):
        def body(kind, s):
            if kind != LAST:
                n = 1 if kind == FIRST else at(s, 2, 0)
                pool.wait_ge(mom_ready, n)
                pool.tensor_tensor(sd[:, 0:1], mom[:, 0, 1:2], half[:, 0:1], ALU.pow).then_inc(sd_ready, 1)
                lay = snap(pool, ((s + 2) % STEPS) // B)
                pool.tensor_copy(gw_pool[:, :], gw_all[:, bass.ds(lay * (4 * K) + 3 * K, 1)]).then_inc(bto_here, 1)
                pool.wait_ge(bto_here, at(s, 1, 1))
                pool.wait_ge(mask_loaded, at(s, 16, 48))
                pool.tensor_tensor(mask[:, :], mask[:, :], gw_pool[:, 0:1].to_broadcast([128, T]), ALU.add).then_inc(mask_summed, 1)
                pool.wait_ge(mask_summed, at(s, 1, 3))
                pool.tensor_tensor(mask[:, :], mask[:, :], half[:, 2:3].to_broadcast([128, T]), ALU.mult).then_inc(mask_ready, 1)
            if kind != FIRST:
                n = at(s, 2, 1) if kind == MID else 2 * s
                pool.wait_ge(mom_ready, n)
                pool.tensor_tensor(sd[:, 1:2], mom[:, 1, 1:2], half[:, 0:1], ALU.pow).then_inc(sd_ready, 1)
                lay = snap(pool, (s - 1) // B)
                pool.tensor_copy(bf1_now[:, :], bf1_t[:, bass.ds(lay * FC, FC)]).then_inc(bf1_ready, 1)
            if kind == LAST:
                pool.wait_ge(mom_ready, 2 * s + 1)
                pool.tensor_tensor(sd[:, 1:2], mom[:, 1, 1:2], half[:, 0:1], ALU.pow).then_inc(sd_ready, 1)

        steps(pool, body)

    @block.tensor
    def _(pe):
        def take_small(kind, s, slot):
            who, n = by_engine(kind, s, slot)
            if who is not None:
                pe.wait_ge(small_out_a if who == "a" else small_out_v, n)

        def scores(kind, s, j):
            if j == 12:
                pe.wait_ge(small_out_v, small_count(kind, s, 0, "v"))
            elif j == 0 and kind != FIRST:
                pe.wait_ge(small_out_v, small_count(kind, s, -1, "v") - 2)
            bcol = snap(pe, (s % B) * T)
            for h in range(2):
                if not (kind == FIRST and j == 0):
                    pe.wait_ge(taken, at(s, 2 * NH, 2 * j - 1 + h))
                for q_part, c_part, c in ((0, 0, 0), (0, 1, 0), (0, 0, 1), (0, 1, 1), (1, 0, 0), (1, 0, 1)):
                    lo = (2 * h + c) * 512
                    mm = pe.matmul(ps_s[:, lo:lo + 512], q_t[:, q_part, j, :],
                                   ctx_t[:, c_part, bass.ds(bcol + lo, 512)],
                                   start=(q_part, c_part) == (0, 0), stop=q_part == 1)
                mm.then_inc(scored, 1)

        def turn(kind, s, j, c):
            if c == 0:
                pe.wait_ge(exp_ready, at(s, NH, j))
            first = kind == FIRST and j == 1
            if c == 0 and not first:
                pe.wait_ge(turned_out_a, chunks_a(s, j - 1, 2))
            if c == 1 and not first:
                if j % 2 == 0:
                    pe.wait_ge(turned_out_a, chunks_a(s, j - 1, 3))
                else:
                    pe.wait_ge(turned_out_v, chunks_v(s, j - 1))
            if c >= 2:
                pe.wait_ge(turned_out_a, chunks_a(s, j, c - 2))
            for i in range(4):
                k = 4 * c + i
                mm = pe.transpose(ps_t[:, c % 2, i * 128:(i + 1) * 128],
                                  probs[:, (j + 1) % 2, k * 128:(k + 1) * 128], ident[:, :])
            mm.then_inc(turned, 1)

        def mix(kind, s, j, i):
            lower = j % 2 == 1
            par = ((j - 3 if lower else j - 4) // 2) % 2
            if i == 0:
                head = j - 3 if lower else j - 4
                if lower:
                    pe.wait_ge(turned_out_a, chunks_a(s, head + 2, 1))
                    if not (kind == FIRST and j == 3):
                        pe.wait_ge(mix_out, at(s, NH // 2, head // 2))
                    if kind != FIRST and j == 3:
                        pe.wait_ge(ctx_lo_in, at(s, 16, 0))
                else:
                    pe.wait_ge(turned_out_a, chunks_a(s, head + 2, 2))
                    pe.wait_ge(turned_out_v, chunks_v(s, head + 2))
                    if kind != FIRST and j == 4:
                        pe.wait_ge(ctx_hi_in, at(s, 16, 0))
            for k in (2 * i, 2 * i + 1):
                k += 0 if lower else NB // 2
                mm = pe.matmul(ps_u[:, 0:256], ctx_n[:, k, :], probs_t[:, par, k * 256:(k + 1) * 256],
                               start=k == 0, stop=k == NB - 1)
            if i == 3:
                mm.then_inc(mixing, 1)

        def project(kind, s, j):
            head = j - 5
            pe.wait_ge(mix_out, at(s, NH // 2, head // 2 + 1))
            if kind != FIRST and j == 5:
                pe.wait_ge(w_value_in, at(s, 16, 0))
            for i in range(2):
                mm = pe.matmul(ps_m[:, i * 128:(i + 1) * 128], mix_t[:, i * 128:(i + 1) * 128],
                               w_value[:, (head + i) % NH, :], start=True, stop=True)
            mm.then_inc(small, 1)

        def queries(kind, s, j, group):
            if kind == MID and j == 4:
                pe.wait_ge(w_score_in, at(s, 16, 0))
            if j == 4:
                pe.wait_ge(small_out_v, small_count(kind, s, 2, "v"))
            for i in range(4):
                mm = pe.matmul(ps_m[:, i * 128:(i + 1) * 128], w_score[:, 4 * group + i, :], x_t[:, :],
                               start=True, stop=True)
            mm.then_inc(small, 1)

        def small_product(kind, s, j):
            if j not in SMALL[kind]:
                return
            take_small(kind, s, j)
            if j % 2 == 1 and j < 20:
                project(kind, s, j)
            elif j == 0:
                queries(kind, s, j, 3)
            elif j in (4, 8, 12):
                queries(kind, s, j, j // 4 - 1)
            elif j == 2:
                pe.wait_ge(xn_ready, at(s, 1, 1))
                pe.transpose(ps_m[:, 0:128], x_n[:, :], ident[:, :]).then_inc(small, 1)
            elif j in (6, 20):
                pe.wait_ge(fn_ready, s + (j == 20))
                pe.transpose(ps_m[:, 0:128], f_n[:, :], ident[:, :]).then_inc(small, 1)
            elif j in (10, 21):
                pe.wait_ge(ffn_in, at(s, 48, 0))
                pe.wait_ge(small_out_v, small_count(kind, s, 6 if j == 10 else 20, "v"))
                for c in range(FC):
                    mm = pe.matmul(ps_m[:, c * 128:(c + 1) * 128], wf1[:, c * 128:(c + 1) * 128], f_t[:, :],
                                   start=True, stop=True)
                mm.then_inc(small, 1)
            elif j in (14, 22):
                pe.wait_ge(small_out_a, small_count(kind, s, 10 if j == 14 else 21, "a"))
                for c in range(FC):
                    pe.matmul(ps_m[:, 0:128], hid_t[:, c * 128:(c + 1) * 128], wf2[:, c, :], start=c == 0, stop=False)
                pe.matmul(ps_m[:, 0:128], ones[0:1, :], bf2[0:1, :], start=False, stop=True).then_inc(small, 1)

        def body(kind, s):
            for j in slots(kind):
                if j < NH:
                    scores(kind, s, j)
                for i in range(4):
                    if (kind != FIRST or j >= 1) and j <= NH:
                        turn(kind, s, j, i)
                    if (kind != FIRST or j >= 3) and j <= NH + 2:
                        mix(kind, s, j, i)
                    if i == 1:
                        small_product(kind, s, j)

        steps(pe, body)

    @block.scalar
    def _(act):
        def unit_of(kind, s, nxt, k):
            n = at(s, K, nxt * K + k)
            bcol = snap(act, ((s + nxt) % B) * T)
            act.activation(unit[:, k % 2, :], side[:, bass.ds(bcol, T)], ACT.Relu,
                           scale=gw_act[:, k:k + 1], bias=gw_act[:, K + k:K + k + 1]).then_inc(unit_ready, 1)

        def chunk_out(kind, s, j, c, extra=()):
            for x_sem, v in extra:
                act.wait_ge(x_sem, v)
            act.wait_ge(turned, at(s, 4 * NH, 4 * (j - 1) + c + 1))
            dst = probs_t[:, ((j + 1) // 2 + 1) % 2, :].rearrange("p (k h f) -> p k h f", k=NB, h=2)
            act.activation(dst[:, 4 * c:4 * c + 4, (j + 1) % 2, :],
                           ps_t[:, c % 2, :].rearrange("p (k f) -> p k f", k=4), ACT.Copy).then_inc(turned_out_a, 1)

        def body(kind, s):
            for j in slots(kind):
                turning = (kind != FIRST or j >= 1) and j <= NH
                more = kind != LAST
                free = [(bias_added, at(s, K, K + 2 * j))] if more else []
                if turning:
                    chunk_out(kind, s, j, 0, free)
                elif free:
                    act.wait_ge(*free[0])
                if more:
                    unit_of(kind, s, 1, 2 * j + 1)
                if turning:
                    chunk_out(kind, s, j, 1)
                if more and j == NH - 1:
                    act.wait_ge(unit_ready, at(s, K, 2 * K))
                if j < NH:
                    act.wait_ge(max_ready, at(s, NH, j + 1))
                    act.activation(probs[:, j % 2, :], probs[:, j % 2, :], ACT.Exp, bias=negmax[:, j % 2:j % 2 + 1],
                                   accum_out=sums[:, j:j + 1]).then_inc(exp_ready, 1)
                if more and j == NH - 1:
                    lay = snap(act, ((s + 2) % STEPS) // B)
                    act.activation(gw_act[:, :], gw_all[:, bass.ds(lay * (4 * K), 2 * K)], ACT.Copy).then_inc(gw_act_ready, 1)
                if j in SMALL[kind] and (SMALL[kind][j] == "a" or j in QUERY_SLOTS):
                    act.wait_ge(small, small_count(kind, s, j))
                    if j in (10, 21):
                        act.wait_ge(bf1_ready, s)
                        for c in range(FC):
                            ins = act.activation(hid_t[:, c * 128:(c + 1) * 128], ps_m[:, c * 128:(c + 1) * 128],
                                                 ACT.Relu, bias=bf1_now[:, c:c + 1])
                        ins.then_inc(small_out_a, 1)
                    else:
                        group = QUERY_SLOTS.index(j)
                        act.activation(q_t[:, 0, 4 * group:4 * group + 4, :],
                                       ps_m[:, :].rearrange("p (n f) -> p n f", n=4), ACT.Copy).then_inc(upper_ready, 1)
                free = [(bias_added, at(s, K, K + 2 * j + 1))] if more else []
                if more and j == NH - 1:
                    free.append((gw_act_ready, at(s, 1, 1)))
                if turning:
                    chunk_out(kind, s, j, 2, free)
                elif free:
                    act.wait_ge(*free[0])
                if more:
                    unit_of(kind, s, 1 if j < NH - 1 else 2, (2 * j + 2) % K)
                if turning and j % 2 == 1:
                    chunk_out(kind, s, j, 3)
                if j % 2 == 0 and (kind != FIRST or j >= 4) and j <= NH + 2:
                    act.wait_ge(mixing, at(s, NH, j - 2))
                    act.activation(mix_t[:, :], ps_u[:, 0:256], ACT.Copy).then_inc(mix_out, 1)

        steps(act, body)

    @block.vector
    def _(dve):
        TOTALS = 5 + 2 * 6, 5 + 2 * 8 + 4

        def body(kind, s):
            done = [0]
            total_first, total_mid = TOTALS

            def count():
                if kind == FIRST:
                    return done[0]
                if kind == MID:
                    return (s - 1) * total_mid + (total_first + done[0])
                return total_first + (STEPS - 2) * total_mid + done[0]

            def chain(ins):
                ins.then_inc(dve_step, 1)
                done[0] += 1
                return ins

            def settle():
                dve.wait_ge(dve_step, count())

            def normalise(w, src, dst, ready):
                chain(dve.tensor_scalar(rs[:, w:w + 1], sd[:, w:w + 1], NORM_EPS, None, ALU.add))
                settle()
                chain(dve.reciprocal(rs[:, w:w + 1], rs[:, w:w + 1]))
                settle()
                dve.tensor_scalar(dst[:, :], src[:, :], mom[:, w, 0:1], rs[:, w:w + 1],
                                  ALU.subtract, ALU.mult).then_inc(ready, 1)

            def add_unit(k):
                dve.wait_ge(unit_ready, at(s, K, K + k + 1))
                dve.wait_ge(bias_added, at(s, K, K + k))
                if k == 0:
                    dve.wait_ge(mask_ready, at(s, 1, 2))
                dve.scalar_tensor_tensor(out=(bias if k == K - 1 else bias_sum)[:, :], in0=unit[:, k % 2, :],
                                         scalar=gw_dve[:, k:k + 1], in1=(mask if k == 0 else bias_sum)[:, :],
                                         op0=ALU.mult, op1=ALU.add).then_inc(bias_added, 1)

            def moments_of(w, rows, column):
                chain(dve.bn_stats(st[:, w, :], rows[:, :]))
                settle()
                dve.memset(pace[:, column:column + 1], 0.0)
                dve.bn_aggr(mom[:, w, :], st[:, w, :]).then_inc(mom_ready, 1)

            def add_head(j, i):
                head = (j - 5) % NH
                src = ps_m[:, i * 128:(i + 1) * 128]
                settle()
                dve.wait_ge(small, small_count(kind, s, j))
                if i == 1:
                    dve.scalar_tensor_tensor(out=y_sum[:, :], in0=src, scalar=rsum[:, 1:2],
                                             in1=y_sum[:, :], op0=ALU.mult, op1=ALU.add).then_inc(small_out_v, 1)
                elif head == 0:
                    chain(dve.tensor_scalar(y_sum[:, :], src, rsum[:, 0:1], None, ALU.mult))
                else:
                    chain(dve.scalar_tensor_tensor(out=y_sum[:, :], in0=src, scalar=rsum[:, 0:1],
                                                   in1=y_sum[:, :], op0=ALU.mult, op1=ALU.add))

            for j in slots(kind):
                with_small = SMALL[kind].get(j) == "v"
                adds_heads = with_small and j % 2 == 1 and j < 20
                if adds_heads:
                    head = (j - 5) % NH
                    dve.wait_ge(exp_ready, at(s, NH, j - 3))
                    if j != 5 or kind != FIRST:
                        dve.wait_ge(small_out_v, small_count(kind, s, j - 1, "v"))
                    chain(dve.reciprocal(rsum[:, :], sums[:, head:head + 2]))
                if j < NH:
                    for h in range(2):
                        if h == 0 and not (kind == FIRST and j < 2):
                            dve.wait_ge(turned, at(s, 4 * NH, 4 * j - 4))
                        dve.wait_ge(scored, at(s, 2 * NH, 2 * j + 1 + h))
                        if h == 0 and not (kind == FIRST and j == 0):
                            dve.wait_ge(max_ready, at(s, NH, j))
                        if h == 0 and j == 0 and kind != FIRST:
                            dve.wait_ge(bias_added, at(s, K, K))
                        dve.memset(pace[:, h:h + 1], 0.0)
                        lo, hi = h * (T // 2), (h + 1) * (T // 2)
                        dve.tensor_tensor_reduce(probs[:, j % 2, lo:hi], ps_s[:, lo:hi], bias[:, lo:hi], 1.0 / Q_UP, LOW,
                                                 ALU.add, ALU.max, tops[:, h:h + 1]).then_inc(taken, 1)
                    dve.wait_ge(taken, at(s, 2 * NH, 2 * j + 2))
                    dve.tensor_scalar(negmax[:, j % 2:j % 2 + 1], tops[:, 0:1], tops[:, 1:2], -1.0,
                                      ALU.max, ALU.mult).then_inc(max_ready, 1)
                if kind != LAST and j == 0:
                    lay = snap(dve, ((s + 1) % STEPS) // B)
                    chain(dve.tensor_scalar(gw_dve[:, :], gw_all[:, bass.ds(lay * (4 * K) + 2 * K, K)], 1.0, None,
                                            ALU.mult))
                    bn = snap(dve, ((s + 1) % B) * D)
                    chain(dve.tensor_scalar(x_now[:, :], x_all[:, :, :].rearrange("p b d -> p (b d)")[:, bass.ds(bn, D)],
                                            1.0, None, ALU.mult))
                    settle()
                if kind != LAST:
                    add_unit(2 * j)
                if kind != LAST and j == 0:
                    moments_of(0, x_now, 2)
                if kind != LAST and j == 1:
                    dve.wait_ge(sd_ready, 1 if kind == FIRST else at(s, 2, 0))
                    normalise(0, x_now, x_n, xn_ready)
                if kind != FIRST and j == 5:
                    dve.wait_ge(sd_ready, at(s, 2, 1) if kind == MID else 2 * s)
                    normalise(1, x_mid, f_n, fn_ready)
                if adds_heads:
                    add_head(j, 0)
                elif with_small and j not in QUERY_SLOTS:
                    dve.wait_ge(small, small_count(kind, s, j))
                    if j in (2, 6, 20):
                        dve.tensor_copy((x_t if j == 2 else f_t)[:, :], ps_m[:, 0:128]).then_inc(small_out_v, 1)
                    else:
                        bp = snap(dve, ((s + (3 if j == 14 else 0)) % B) * D)
                        dve.tensor_tensor(x_all[:, :, :].rearrange("p b d -> p (b d)")[:, bass.ds(bp, D)],
                                          ps_m[:, 0:128], x_mid[:, :], ALU.add).then_inc(small_out_v, 1)
                if kind != LAST:
                    add_unit(2 * j + 1)
                if adds_heads:
                    add_head(j, 1)
                if j in (3, 19) and adds_heads:
                    dve.wait_ge(small_out_v, small_count(kind, s, j, "v"))
                    bp = snap(dve, ((s + (3 if j == 3 else 0)) % B) * D)
                    chain(dve.tensor_tensor(x_mid[:, :], x_all[:, :, :].rearrange("p b d -> p (b d)")[:, bass.ds(bp, D)],
                                            y_sum[:, :], ALU.add))
                    settle()
                    moments_of(1, x_mid, 3)
                    if j == 19:
                        dve.wait_ge(sd_ready, 2 * s + 1)
                        normalise(1, x_mid, f_n, fn_ready)
                if j % 2 == 0 and (kind != FIRST or j >= 1) and j <= NH:
                    dve.wait_ge(turned, at(s, 4 * NH, 4 * j))
                    dst = probs_t[:, ((j + 1) // 2 + 1) % 2, :].rearrange("p (k h f) -> p k h f", k=NB, h=2)
                    dve.tensor_copy(dst[:, 12:16, (j + 1) % 2, :],
                                    ps_t[:, 1, :].rearrange("p (k f) -> p k f", k=4)).then_inc(turned_out_v, 1)
                if with_small and j in QUERY_SLOTS:
                    group = QUERY_SLOTS.index(j)
                    heads = slice(4 * group, 4 * group + 4)
                    dve.wait_ge(upper_ready, at(s, 4, 1 + sorted(QUERY_SLOTS).index(j)))
                    dve.tensor_tensor(q_t[:, 1, heads, :], ps_m[:, :].rearrange("p (n f) -> p n f", n=4),
                                      q_t[:, 0, heads, :], ALU.subtract).then_inc(small_out_v, 1)
            return done[0]

        assert body(FIRST, 0) == TOTALS[0]
        with dve.Fori(1, STEPS - 1) as s:
            assert body(MID, s) == TOTALS[1]
        body(LAST, STEPS - 1)


def prologue(nc, a, mem, sem, sbuf, psum, v):
    x_all, ident, ones, half = v["x_all"], v["ident"], v["ones"], v["half"]
    stats, moments, dev, rdev = v["stats"], v["moments"], v["dev"], v["rdev"]
    ctx_t, side, ctx_n, q_t, w_score, w_value = (v[n] for n in ("ctx_t", "side", "ctx_n", "q_t", "w_score", "w_value"))
    bias, bias_sum, unit, mask, gw_all, gw_act, gw_dve, gw_pool = (
        v[n] for n in ("bias", "bias_sum", "unit", "mask", "gw_all", "gw_act", "gw_dve", "gw_pool"))
    x_t, x_n, x_now, bf1_t = v["x_t"], v["x_n"], v["x_now"], v["bf1_t"]
    unit_ready, bias_added, mask_loaded, mask_ready = (v[n] for n in ("unit_ready", "bias_added", "mask_loaded", "mask_ready"))
    mask_summed = v["mask_summed"]
    score_dram, value_dram = v["score_dram"], v["value_dram"]
    weights = [a["L0_xattn_W" + n].rearrange("l d n h -> l d (n h)") for n in "qkv"]
    wo_dram = a["L0_xattn_Wo"].rearrange("l n h d -> l (n h) d").rearrange("l (c p) d -> l p c d", p=128)

    with ExitStack() as tmp:
        raw = sbuf(tmp, "raw", [128, 2, 4 * NH * HD])
        w_t = sbuf(tmp, "w_t", [128, 3, NH // 2, 128])
        bf1_rows = sbuf(tmp, "bf1_rows", [L * FC, 128])
        ps = psum(tmp, "ps_pro", [128, 8, 512])

        filled = sem("filled")
        emptied_a, emptied_v = sem("emptied_a"), sem("emptied_v")
        x_in, gw_in, bf1_in = sem("x_in"), sem("gw_in"), sem("bf1_in")
        side_in = [sem(f"side_in{b}") for b in range(B)]
        raw_in = [sem(f"raw_in{i}") for i in range(2)]
        ctx_in = sem("ctx_in")
        merged_out = sem("score_weights_out"), sem("value_weights_out")
        consts, rows, powed, gw_own = sem("consts"), sem("rows"), sem("powed"), sem("gw_own")
        pro_gw_act = sem("pro_gw_act")
        mask_used = sem("mask_used")
        uppers = sem("uppers")

        fills = []
        for i in range(L):
            fills += [("turn_w", i, w, c) for w in range(3) for c in range(2)]
            fills += [("turn_c", i, 0, c) for c in range(4)]
            fills += [("merge", i, w, c) for w in range(2) for c in range(4)]
        fills += [("turn_b", 0, 0, 0), ("turn_x", 0, 0, 0)] + [("query", 0, 0, c) for c in range(3)]
        where = {f: i for i, f in enumerate(fills)}

        split = [f[0] in ("turn_c", "query") for f in fills]
        by_vector = [split[i] or i % 5 == 1 for i in range(len(fills))]

        def emptied(eng, i):
            eng.wait_ge(emptied_v if by_vector[i] else emptied_a, by_vector[:i + 1].count(by_vector[i]))

        block = tmp.enter_context(nc.Block())

        @block.sync
        def _(sp):
            def store(i):
                for w, dst in enumerate((score_dram, value_dram)):
                    for c in range(4):
                        emptied(sp, where[("merge", i, w, c)])
                    sp.dma_start(dst[L - 1 - i], (w_score, w_value)[w][:, :, :]).then_inc(merged_out[w], 16)

            gw = gw_all[:, :].rearrange("p (l n) -> p l n", l=L)
            for n, name in enumerate(("Wth", "bth", "Wto")):
                src = a["L0_xattn_" + name]
                if name == "Wth":
                    src = src.rearrange("l i k -> l (i k)")
                elif name == "Wto":
                    src = src.rearrange("l k i -> l (k i)")
                sp.dma_start(gw[:, :, n * K:(n + 1) * K], src.unsqueeze(0).to_broadcast([128, L, K])).then_inc(gw_in, 16)
            for l in range(L):
                sp.dma_start(gw[:, l, 3 * K:3 * K + 1], a["L0_xattn_bto"][l:l + 1, :].to_broadcast([128, 1])).then_inc(gw_in, 16)
            sp.dma_start(side[:, 0:T], v["side_dram"][0]).then_inc(side_in[0], 16)
            sp.dma_start(x_all[:, :, :], v["x_dram"]).then_inc(x_in, 16)
            sp.dma_start(mask[:, :], v["mask_dram"][0:1, :].to_broadcast([128, T])).then_inc(mask_loaded, 16)
            sp.dma_start(bf1_rows[:, :], a["L0_xattn_bf1"].rearrange("l (c p) -> (l c) p", p=128)).then_inc(bf1_in, 16)
            for i in range(L):
                lay = L - 1 - i
                if i >= 2:
                    store(i - 2)
                    sp.wait_ge(filled, where[("merge", i - 2, 1, 3)] + 1)
                for w in range(3):
                    sp.dma_start(raw[:, i % 2, w * 1024:(w + 1) * 1024], weights[w][lay]).then_inc(raw_in[i % 2], 16)
                sp.dma_start(raw[:, i % 2, 3072:4096].rearrange("p (c d) -> p c d", d=128), wo_dram[lay]).then_inc(raw_in[i % 2], 16)
                if i >= 1:
                    sp.wait_ge(filled, where[("turn_c", i - 1, 0, 3)] + 1)
                sp.dma_start(ctx_n[:, :, :], v["ctx_dram"][B - 1 - i]).then_inc(ctx_in, 16)
                if i == 1:
                    sp.wait_ge(mask_used, 1)
                    sp.dma_start(mask[:, :], v["mask_dram"][1:2, :].to_broadcast([128, T])).then_inc(mask_loaded, 16)
                    for b in range(1, B):
                        sp.dma_start(side[:, b * T:(b + 1) * T], v["side_dram"][b]).then_inc(side_in[b], 16)
            for i in (2, 3):
                store(i)
            for w in range(2):
                sp.wait_ge(merged_out[w], 16 * L)
            for b in range(2, B):
                sp.wait_ge(side_in[b], 16)

        @block.gpsimd
        def _(pool):
            pool.memset(ident[:, :], 0.0).then_inc(consts, 1)
            pool.memset(ones[:, :], 1.0).then_inc(consts, 1)
            pool.memset(half[:, 0:1], 0.5).then_inc(consts, 1)
            pool.memset(half[:, 1:2], -0.5).then_inc(consts, 1)
            pool.memset(half[:, 2:3], Q_UP).then_inc(consts, 1)
            pool.wait_ge(consts, 5)
            pool.affine_select(out=ident[:, :], in_=ident[:, :], compare_op=ALU.not_equal, fill=1.0, base=0,
                               pattern=[[-1, 128]], channel_multiplier=1).then_inc(consts, 1)
            pool.wait_ge(gw_in, 16 * (3 + L))
            def add_bto(n):
                pool.wait_ge(mask_loaded, 16 * (n + 1))
                pool.tensor_tensor(mask[:, :], mask[:, :], gw_all[:, 3 * K:3 * K + 1].to_broadcast([128, T]),
                                   ALU.add).then_inc(mask_summed, 1)
                pool.wait_ge(mask_summed, n + 1)
                pool.tensor_tensor(mask[:, :], mask[:, :], half[:, 2:3].to_broadcast([128, T]),
                                   ALU.mult).then_inc(mask_ready, 1)

            pool.wait_ge(rows, 1)
            pool.tensor_tensor(rdev[:, :], dev[:, :], half[:, 1:2].to_broadcast([128, B]), ALU.pow).then_inc(powed, 1)
            add_bto(0)
            pool.wait_ge(rows, 2)
            pool.tensor_tensor(dev[:, 0:1], moments[:, 0, 1:2], half[:, 0:1], ALU.pow).then_inc(powed, 1)
            add_bto(1)

        @block.tensor
        def _(pe):
            pe.wait_ge(consts, 6)
            for n, (what, i, w, c) in enumerate(fills):
                if n >= 8:
                    emptied(pe, n - 8)
                bank = ps[:, n % 8, :]
                if what == "turn_w":
                    if (w, c) == (0, 0):
                        pe.wait_ge(raw_in[i % 2], 64 * (i // 2 + 1))
                    for k in range(4):
                        lo = w * 1024 + (4 * c + k) * 128
                        mm = pe.transpose(bank[:, k * 128:(k + 1) * 128], raw[:, i % 2, lo:lo + 128], ident[:, :])
                elif what == "turn_c":
                    if c == 0:
                        pe.wait_ge(ctx_in, 16 * (i + 1))
                    for k in range(4):
                        mm = pe.transpose(bank[:, k * 128:(k + 1) * 128], ctx_n[:, 4 * c + k, :], ident[:, :])
                elif what == "merge":
                    if (w, c) == (0, 0):
                        for k in range(6):
                            emptied(pe, where[("turn_w", i, k // 2, k % 2)])
                    odd, part = c // 2, c % 2
                    rows_ = slice(64 * odd, 64 * odd + 64)
                    for k in range(4):
                        pair = 4 * part + k
                        if w == 0:
                            lhs, rhs = w_t[rows_, 0, pair, :], w_t[rows_, 1, pair, :]
                        else:
                            lhs = w_t[rows_, 2, pair, :]
                            rhs = raw[rows_, i % 2, 3072 + pair * 128:3072 + (pair + 1) * 128]
                        mm = pe.matmul(bank[:, k * 128:(k + 1) * 128], lhs, rhs, start=True, stop=True)
                elif what == "turn_b":
                    pe.wait_ge(bf1_in, 16)
                    mm = pe.transpose(bank[:, 0:L * FC], bf1_rows[:, :], ident[0:L * FC, 0:L * FC])
                elif what == "turn_x":
                    pe.wait_ge(rows, 3)
                    mm = pe.transpose(bank[:, 0:128], x_n[:, :], ident[:, :])
                else:
                    if c == 0:
                        emptied(pe, where[("turn_x", 0, 0, 0)])
                        for k in range(4):
                            emptied(pe, where[("merge", L - 1, 0, k)])
                    for k in range(4):
                        mm = pe.matmul(bank[:, k * 128:(k + 1) * 128], w_score[:, 4 * c + k, :], x_t[:, :],
                                       start=True, stop=True)
                mm.then_inc(filled, 1)

        def empty(eng, n, vector):
            what, i, w, c = fills[n]
            bank = ps[:, n % 8, :]
            eng.wait_ge(filled, n + 1)
            scale = 1.0
            if what == "turn_w":
                if i >= 1 and (w, c) in ((0, 0), (0, 1)):
                    eng.wait_ge(filled, where[("merge", i - 1, 1, 3)] + 1)
                if w == 0:
                    scale = float(HD) ** -0.5 * Q_UP
                dst, src = w_t[:, w, 4 * c:4 * c + 4, :], bank.rearrange("p (k f) -> p k f", k=4)
            elif what == "turn_c":
                lo = (B - 1 - i) * T + c * 512
                dst, src = ctx_t[:, int(vector), lo:lo + 512], bank
                upper = ctx_t[:, 0, lo:lo + 512]
            elif what == "merge":
                if i >= 1:
                    eng.wait_ge(merged_out[w], 16 * i)
                odd, part = c // 2, c % 2
                dst = (w_score, w_value)[w][:, :, :].rearrange("p (m two) d -> p m two d", two=2)[:, 4 * part:4 * part + 4, odd, :]
                src = bank.rearrange("p (k f) -> p k f", k=4)
            elif what == "turn_b":
                dst, src = bf1_t[:, :], bank[:, 0:L * FC]
            elif what == "turn_x":
                dst, src = x_t[:, :], bank[:, 0:128]
            else:
                dst, src = q_t[:, int(vector), 4 * c:4 * c + 4, :], bank.rearrange("p (k f) -> p k f", k=4)
                upper = q_t[:, 0, 4 * c:4 * c + 4, :]
            if split[n] and vector:
                eng.wait_ge(uppers, split[:n + 1].count(True))
                eng.tensor_tensor(dst, src, upper, ALU.subtract).then_inc(emptied_v, 1)
            elif split[n]:
                eng.activation(dst, src, ACT.Copy).then_inc(uppers, 1)
            elif vector:
                eng.tensor_scalar(dst, src, scale, None, ALU.mult).then_inc(emptied_v, 1)
            else:
                eng.activation(dst, src, ACT.Copy, scale=scale).then_inc(emptied_a, 1)

        mine = ([n for n in range(len(fills)) if split[n] or not by_vector[n]],
                [n for n in range(len(fills)) if by_vector[n]])

        def due(n, k):
            return n * (K - 5) < (k - 3) * len(fills)

        @block.scalar
        def _(act):
            act.wait_ge(gw_in, 16 * (3 + L))
            act.activation(gw_act[:, :], gw_all[:, 0:2 * K], ACT.Copy).then_inc(pro_gw_act, 1)
            act.wait_ge(pro_gw_act, 1)
            act.wait_ge(side_in[0], 16)
            nf = 0
            for k in range(K + 1):
                if k >= 2:
                    act.wait_ge(bias_added, k - 1)
                if k == K:
                    act.wait_ge(side_in[1], 16)
                src = side[:, (k // K) * T:(k // K + 1) * T]
                act.activation(unit[:, k % 2, :], src, ACT.Relu, scale=gw_act[:, k % K:k % K + 1],
                               bias=gw_act[:, K + k % K:K + k % K + 1]).then_inc(unit_ready, 1)
                while nf < len(mine[0]) and due(mine[0][nf], k):
                    empty(act, mine[0][nf], False)
                    nf += 1

        @block.vector
        def _(dve):
            n_own = [0]

            def own(ins):
                ins.then_inc(gw_own, 1)
                n_own[0] += 1
                dve.wait_ge(gw_own, n_own[0])

            dve.wait_ge(x_in, 16)
            for b in range(B):
                own(dve.bn_stats(stats[:, b, :], x_all[:, b, :]))
                own(dve.bn_aggr(moments[:, b, :], stats[:, b, :]))
            dve.tensor_scalar(dev[:, :], moments[:, :, 1], LN_EPS, None, ALU.add).then_inc(rows, 1)
            dve.wait_ge(gw_in, 16 * (3 + L))
            wto = gw_all[:, :].rearrange("p (l n) -> p l n", l=L)[:, :, 2 * K:3 * K]
            own(dve.tensor_scalar(wto, wto, Q_UP, None, ALU.mult))
            own(dve.tensor_copy(gw_dve[:, :], gw_all[:, 2 * K:3 * K]))
            nf = 0
            for k in range(K):
                dve.wait_ge(unit_ready, k + 1)
                if k == 0:
                    dve.tensor_scalar(bias_sum[:, :], unit[:, 0, :], gw_dve[:, 0:1], None, ALU.mult).then_inc(bias_added, 1)
                else:
                    dve.wait_ge(bias_added, k)
                    dve.scalar_tensor_tensor(out=(bias if k == K - 1 else bias_sum)[:, :], in0=unit[:, k % 2, :],
                                             scalar=gw_dve[:, k:k + 1], in1=bias_sum[:, :],
                                             op0=ALU.mult, op1=ALU.add).then_inc(bias_added, 1)
                if k == 4:
                    dve.wait_ge(mask_ready, 1)
                    dve.wait_ge(bias_added, k + 1)
                    dve.tensor_tensor(bias_sum[:, :], bias_sum[:, :], mask[:, :], ALU.add).then_inc(mask_used, 1)
                    dve.wait_ge(mask_used, 1)
                if k == 1:
                    dve.wait_ge(powed, 1)
                    for b in range(B):
                        own(dve.tensor_scalar(x_all[:, b, :], x_all[:, b, :], moments[:, b, 0:1], rdev[:, b:b + 1],
                                              ALU.subtract, ALU.mult))
                    own(dve.bn_stats(stats[:, 0, :], x_all[:, 0, :]))
                    dve.bn_aggr(moments[:, 0, :], stats[:, 0, :]).then_inc(rows, 1)
                if k == 6:
                    dve.wait_ge(powed, 2)
                    dve.wait_ge(rows, 2)
                    own(dve.tensor_scalar(dev[:, 0:1], dev[:, 0:1], NORM_EPS, None, ALU.add))
                    own(dve.reciprocal(rdev[:, 0:1], dev[:, 0:1]))
                    dve.tensor_scalar(x_n[:, :], x_all[:, 0, :], moments[:, 0, 0:1], rdev[:, 0:1],
                                      ALU.subtract, ALU.mult).then_inc(rows, 1)
                while nf < len(mine[1]) and due(mine[1][nf], k):
                    empty(dve, mine[1][nf], True)
                    nf += 1


def self_attention_and_experts(nc, a, out, top, mem, sem, sbuf, psum, v):
    x_all, ident, ones, half = v["x_all"], v["ident"], v["ones"], v["half"]
    stats, moments, dev, rdev = v["stats"], v["moments"], v["dev"], v["rdev"]
    x_in0 = sbuf(mem, "x_in0", [128, B, D])
    w_q = sbuf(mem, "w_q", [128, 4, 4, 32])
    w_k = sbuf(mem, "w_k", [128, 4, 4, 32])
    w_v = sbuf(mem, "w_v", [128, SH, SK])
    w_o = sbuf(mem, "w_o", [128, 128])
    b_q = sbuf(mem, "b_q", [128, 4])
    b_k = sbuf(mem, "b_k", [128, 4])
    b_q_rows = sbuf(mem, "b_q_rows", [4, 4, 32])
    b_k_rows = sbuf(mem, "b_k_rows", [4, 4, 32])
    b_v = sbuf(mem, "b_v", [1, 128])
    b_o = sbuf(mem, "b_o", [1, 128])
    causal = sbuf(mem, "causal", [128, 128])
    gate = sbuf(mem, "gate", [NE, D])
    gate_t = sbuf(mem, "gate_t", [128, NE])
    w1 = sbuf(mem, "w1", [128, NE, FILT])
    w2 = sbuf(mem, "w2", [128, NE * FC, D])
    b1 = sbuf(mem, "b1", [NE * FC, 128])
    b1_t = sbuf(mem, "b1_t", [128, NE * FC])
    b2 = sbuf(mem, "b2", [NE, D])
    gate_w_t = sbuf(mem, "gate_w_t", [NE, B * F])
    index = sbuf(mem, "index", [128, B, NE])
    xn = sbuf(mem, "xn", [128, B, D])
    xn_t = sbuf(mem, "xn_t", [128, B * F])
    qh = sbuf(mem, "qh", [128, 4, B * F])
    kh = sbuf(mem, "kh", [128, 4, B * F])
    v_wide = sbuf(mem, "v_wide", [128, B * SH * 128 + 128])
    att = sbuf(mem, "att", [128, 2, SH, F])
    att_t = sbuf(mem, "att_t", [128, SH, F])
    peak = sbuf(mem, "peak", [128, SH])
    negpeak = sbuf(mem, "negpeak", [128, 2, SH])
    total = sbuf(mem, "total", [128, 2, SH])
    rtotal = sbuf(mem, "rtotal", [128, SH])
    mixed_t = sbuf(mem, "mixed_t", [128, 128])
    hid = sbuf(mem, "hid", [128, 2, FC, B * F])
    y = sbuf(mem, "y", [128, B, D])
    g = {n: sbuf(mem, "gate_" + n, [128, B, NE]) for n in ("z", "p", "m", "c", "one", "two", "left", "w")}
    g1 = {n: sbuf(mem, "gcol_" + n, [128, B]) for n in ("top", "sum", "best", "pick", "second", "pick2")}

    ps_a = psum(mem, "ps_a", [128, 4, 512])
    ps_b = psum(mem, "ps_b", [128, 4, 512])

    x_in, att_in, v_in, moe_in = sem("x0_in"), sem("att_in"), sem("v_in"), sem("moe_in")
    zeroed, masked = sem("zeroed"), sem("masked")
    ve_step, dev_in, powed2 = sem("ve_step"), sem("dev_in"), sem("powed2")
    first_norm, rows_n = sem("first_norm"), sem("rows_n")
    pa, pa_out_a, pa_out_v = sem("pa"), sem("pa_out_a"), sem("pa_out_v")
    s_ready, s_shift, s_exp, t_ready, t_out = sem("s_ready"), sem("s_shift"), sem("s_exp"), sem("t_ready"), sem("t_out")
    s_taken = sem("s_taken")
    s_scaled, m_ready, m_out, o_ready, o_out = (sem(n) for n in ("s_scaled", "m_ready", "m_out", "o_ready", "o_out"))
    x_t2, x_t2_out, gl_ready, gl_out, gexp = (sem(n) for n in ("x_t2", "x_t2_out", "gl_ready", "gl_out", "gexp"))
    h_ready, h_out, y_ready, y_out, stored = (sem(n) for n in ("h_ready", "h_out", "y_ready", "y_out", "stored"))
    w_ready, wt_ready, wt_out, bias_ready = (sem(n) for n in ("w_ready", "wt_ready", "wt_out", "bias_ready"))
    gshift, bt_ready, bt_out = sem("gshift"), sem("bt_ready"), sem("bt_out")

    block = mem.enter_context(nc.Block())

    def load_queries_or_keys(eng, w, b, n):
        eng.wait_ge(zeroed, 4)
        for c in range(4):
            eng.dma_start(w[:, c, :, 0:SK], a["L0_attn_W" + n][4 * c:4 * c + 4].rearrange("h d k -> d h k")).then_inc(att_in, 16)
        eng.dma_start(b[:, :, 0:SK], a["L0_attn_b" + n].rearrange("(c j) k -> c j k", j=4)).then_inc(att_in, 16)

    @block.sync
    def _(sp):
        sp.dma_start(x_in0[:, :, :], v["x_dram"]).then_inc(x_in, 16)
        load_queries_or_keys(sp, w_q, b_q_rows, "q")
        for e in range(NE):
            sp.dma_start(w1[:, e, :], a["L0_ffn_w1"][e]).then_inc(moe_in, 16)
            sp.dma_start(w2[:, e * FC:(e + 1) * FC, :], a["L0_ffn_w2"][e].rearrange("(c p) d -> p c d", p=128)).then_inc(moe_in, 16)
        sp.dma_start(b2[:, :], a["L0_ffn_b2"]).then_inc(moe_in, 16)
        sp.wait_ge(y_out, NE)
        sp.dma_start(out.rearrange("b f d -> f b d"), y[:, :, :]).then_inc(stored, 16)
        sp.wait_ge(stored, 16)

    ATT_IN = 16 * (2 + 2 * 5)

    @block.gpsimd
    def _(pool):
        for t in (w_q, w_k):
            pool.memset(t[:, :, :, :], 0.0).then_inc(zeroed, 1)
        for t in (b_q_rows, b_k_rows):
            pool.memset(t[:, :, :], 0.0).then_inc(zeroed, 1)
        pool.memset(causal[:, :], 0.0).then_inc(masked, 1)
        pool.wait_ge(masked, 1)
        pool.affine_select(out=causal[:, :], in_=causal[:, :], compare_op=ALU.is_ge, fill=NEG, base=0,
                           pattern=[[-1, 128]], channel_multiplier=1).then_inc(masked, 1)
        for e in range(NE):
            pool.memset(index[:, :, e], float(e)).then_inc(masked, 1)
        for n in range(3):
            pool.wait_ge(dev_in, n + 1)
            pool.tensor_tensor(rdev[:, :], dev[:, :], half[:, (n > 0):(n > 0) + 1].to_broadcast([128, B]),
                               ALU.pow).then_inc(powed2, 1)
            if n == 1:
                pool.memset(v_wide[:, :], 0.0).then_inc(zeroed, 1)

    @block.tensor
    def _(pe):
        def keep_warm(n, bank):
            for _ in range(n):
                pe.matmul(ps_b[:, bank, 384:512], ident[:, :], ident[:, :], start=True, stop=True)

        keep_warm(26, 3)
        pe.wait_ge(att_in, ATT_IN)
        pe.transpose(ps_b[:, 0, 0:NE], gate[:, :], ident[0:NE, 0:NE])
        for i, t in enumerate((b_q_rows, b_k_rows)):
            pe.transpose(ps_b[:, 2, 4 * i:4 * i + 4], t[:, :, :].rearrange("c j k -> c (j k)"), ident[0:4, 0:4])
        pe.transpose(ps_b[:, 1, 0:NE * FC], b1[:, :], ident[0:NE * FC, 0:NE * FC]).then_inc(bt_ready, 1)
        keep_warm(6, 3)
        pe.wait_ge(rows_n, B)
        for b in range(B):
            mm = pe.transpose(ps_a[:, 0, b * 128:(b + 1) * 128], xn[:, b, :], ident[:, :])
        mm.then_inc(pa, 1)
        pe.wait_ge(pa_out_v, 1)
        n = 0
        for w in (w_q, w_k):
            for c in range(4):
                bank = 1 + n % 3
                if n >= 3:
                    pe.wait_ge(pa_out_a, n - 2)
                pe.matmul(ps_a[:, bank, :], w[:, c, :, :].rearrange("p j k -> p (j k)"), xn_t[:, :],
                          start=True, stop=True).then_inc(pa, 1)
                n += 1
        pe.wait_ge(bt_out, 4)
        pe.wait_ge(v_in, 16 * 4)
        for b in range(B):
            o = ps_a[:, 0, b * 128:(b + 1) * 128]
            pe.matmul(o, xn_t[:, b * 128:(b + 1) * 128], w_v[:, :, :].rearrange("p h k -> p (h k)"),
                      start=b == 0, stop=False, skip_group_check=True)
            mm = pe.matmul(o, ones[0:1, :], b_v[0:1, :], start=False, stop=True, skip_group_check=True)
        mm.then_inc(pa, 1)
        pe.wait_ge(pa_out_a, 8)
        pe.wait_ge(pa_out_v, 2)

        def logits(b):
            if b >= 1:
                pe.wait_ge(s_taken, b)
            for c in range(4):
                for j in range(4):
                    r = slice(32 * j, 32 * j + 32)
                    mm = pe.matmul(ps_a[:, j, c * 128:(c + 1) * 128], qh[r, c, b * 128:(b + 1) * 128],
                                   kh[r, c, b * 128:(b + 1) * 128], start=True, stop=True)
            mm.then_inc(s_ready, 1)

        def turned(b):
            pe.wait_ge(s_scaled, b + 1)
            for q in range(4):
                n = 4 * b + q
                if n >= 3:
                    pe.wait_ge(t_out, n - 2)
                for c in range(4):
                    mm = pe.transpose(ps_b[:, n % 3, c * 128:(c + 1) * 128], att[:, b % 2, 4 * q + c, :], ident[:, :])
                mm.then_inc(t_ready, 1)

        logits(0)
        keep_warm(10, 0)
        logits(1)
        keep_warm(20, 0)
        turned(0)
        for b in range(B):
            if b + 2 < B:
                logits(b + 2)
            pe.wait_ge(t_out, 4 * b + 4)
            if b >= 1:
                pe.wait_ge(o_out, b)
            for h in range(SH):
                real = 4 * (h % 4) + h // 4
                mm = pe.matmul(ps_b[:, 3, 0:128], v_wide[:, (b * SH + real) * 128:(b * SH + real + 1) * 128],
                               att_t[:, h, :], start=h == 0, stop=h == SH - 1)
            mm.then_inc(m_ready, 1)
            if b + 1 < B:
                turned(b + 1)
            pe.wait_ge(m_out, b + 1)
            pe.matmul(ps_b[:, 3, 128:256], mixed_t[:, :], w_o[:, :], start=True, stop=False)
            pe.matmul(ps_b[:, 3, 128:256], ones[0:1, :], b_o[0:1, :], start=False, stop=True).then_inc(o_ready, 1)

        keep_warm(16, 0)
        pe.wait_ge(rows_n, 2 * B)
        for b in range(B):
            mm = pe.transpose(ps_a[:, 0, b * 128:(b + 1) * 128], xn[:, b, :], ident[:, :])
        mm.then_inc(x_t2, 1)
        pe.wait_ge(x_t2_out, 1)
        for b in range(B):
            mm = pe.matmul(ps_b[:, 3, b * NE:(b + 1) * NE], xn_t[:, b * 128:(b + 1) * 128], gate_t[:, :],
                           start=True, stop=True)
        mm.then_inc(gl_ready, 1)
        pe.wait_ge(moe_in, 16 * (2 * NE + 1))

        def hidden(e):
            for c in range(FC):
                n = e * FC + c
                if n >= FC:
                    pe.wait_ge(h_out, n - FC + 1)
                pe.matmul(ps_a[:, c, :], w1[:, e, c * 128:(c + 1) * 128], xn_t[:, :],
                          start=True, stop=True).then_inc(h_ready, 1)

        hidden(0)
        for e in range(NE):
            if e + 1 < NE:
                hidden(e + 1)
            pe.wait_ge(h_out, FC * (e + 1))
            if e >= 2:
                pe.wait_ge(y_out, e - 1)
            for b in range(B):
                o = ps_b[:, e % 2, b * 128:(b + 1) * 128]
                for c in range(FC):
                    mm = pe.matmul(o, hid[:, e % 2, c, b * 128:(b + 1) * 128], w2[:, e * FC + c, :],
                                   start=c == 0, stop=c == FC - 1)
            mm.then_inc(y_ready, 1)
            if e == 3:
                pe.wait_ge(w_ready, 1)
                for b in range(B):
                    mm = pe.transpose(ps_b[0:NE, 3, b * 128:(b + 1) * 128], g["w"][:, b, :], ident[:, :])
                mm.then_inc(wt_ready, 1)
            if e == 4:
                pe.wait_ge(wt_out, 1)
                for b in range(B):
                    mm = pe.matmul(ps_b[:, 2, b * 128:(b + 1) * 128], gate_w_t[:, b * 128:(b + 1) * 128], b2[:, :],
                                   start=True, stop=True)
                mm.then_inc(bias_ready, 1)

    @block.scalar
    def _(act):
        act.dma_start(gate[:, :], a["L0_ffn_gate_w"]).then_inc(att_in, 16)
        act.dma_start(b1[:, :], a["L0_ffn_b1"].rearrange("e (c p) -> (e c) p", p=128)).then_inc(att_in, 16)
        load_queries_or_keys(act, w_k, b_k_rows, "k")
        act.dma_start(w_v[:, :, :], a["L0_attn_Wv"].rearrange("h d k -> d h k")).then_inc(v_in, 16)
        act.dma_start(w_o[:, :], a["L0_attn_Wo"]).then_inc(v_in, 16)
        act.dma_start(b_v[:, :], a["L0_attn_bv"].rearrange("(o h) k -> o (h k)", o=1)).then_inc(v_in, 16)
        act.dma_start(b_o[:, :], a["L0_attn_bo"].rearrange("(o n) -> o n", o=1)).then_inc(v_in, 16)
        n = 0
        act.wait_ge(bt_out, 4)
        for w in range(2):
            for c in range(4):
                act.wait_ge(pa, n + 2)
                act.activation((qh, kh)[w][:, c, :], ps_a[:, 1 + n % 3, :], ACT.Identity,
                               bias=(b_q, b_k)[w][:, c:c + 1]).then_inc(pa_out_a, 1)
                n += 1
        def exponentials(b):
            act.wait_ge(s_shift, b + 1)
            for h in range(SH):
                ins = act.activation(att[:, b % 2, h, :], att[:, b % 2, h, :], ACT.Exp, bias=negpeak[:, b % 2, h:h + 1],
                                     accum_out=total[:, b % 2, h:h + 1])
            ins.then_inc(s_exp, 1)

        exponentials(0)
        exponentials(1)
        for b in range(B):
            if b >= 1:
                act.wait_ge(m_ready, b)
            for q in range(4):
                act.wait_ge(t_ready, 4 * b + q + 1)
                act.activation(att_t[:, 4 * q:4 * q + 4, :].rearrange("p h f -> p (h f)"), ps_b[:, (4 * b + q) % 3, :],
                               ACT.Copy).then_inc(t_out, 1)
            if 1 <= b < B - 1:
                exponentials(b + 1)
        act.wait_ge(gshift, 1)
        act.activation(g["p"][:, :, :], g["z"][:, :, :], ACT.Exp).then_inc(gexp, 1)
        for e in range(NE):
            for c in range(FC):
                n = e * FC + c
                act.wait_ge(h_ready, n + 1)
                if e >= 2:
                    act.wait_ge(y_ready, e - 1)
                act.activation(hid[:, e % 2, c, :], ps_a[:, c, :], ACT.Silu, bias=b1_t[:, n:n + 1]).then_inc(h_out, 1)

    @block.vector
    def _(dve):
        n_own = [0]

        def own(ins):
            ins.then_inc(ve_step, 1)
            n_own[0] += 1
            dve.wait_ge(ve_step, n_own[0])

        def row_moments(b):
            own(dve.bn_stats(stats[:, b, :], x_all[:, b, :]))
            own(dve.bn_aggr(moments[:, b, :], stats[:, b, :]))

        def normalise(ready):
            for b in range(B):
                dve.tensor_scalar(xn[:, b, :], x_all[:, b, :], moments[:, b, 0:1], rdev[:, b:b + 1],
                                  ALU.subtract, ALU.mult).then_inc(ready, 1)

        for b in range(B):
            row_moments(b)
        dve.tensor_copy(dev[:, :], moments[:, :, 1]).then_inc(dev_in, 1)
        dve.wait_ge(powed2, 1)
        own(dve.tensor_scalar(rdev[:, :], rdev[:, :], NORM_EPS, None, ALU.add))
        own(dve.reciprocal(rdev[:, :], rdev[:, :]))
        normalise(first_norm)
        dve.wait_ge(first_norm, B)
        dve.wait_ge(x_in, 16)
        own(dve.tensor_tensor(x_all[:, :, :], xn[:, :, :], x_in0[:, :, :], ALU.add))
        for b in range(B):
            row_moments(b)
        dve.tensor_scalar(dev[:, :], moments[:, :, 1], LN_EPS, None, ALU.add).then_inc(dev_in, 1)
        dve.wait_ge(powed2, 2)
        normalise(rows_n)
        dve.wait_ge(bt_ready, 1)
        dve.tensor_copy(gate_t[:, :], ps_b[:, 0, 0:NE]).then_inc(bt_out, 1)
        dve.tensor_copy(b1_t[:, :], ps_b[:, 1, 0:NE * FC]).then_inc(bt_out, 1)
        dve.tensor_copy(b_q[:, :], ps_b[:, 2, 0:4]).then_inc(bt_out, 1)
        dve.tensor_copy(b_k[:, :], ps_b[:, 2, 4:8]).then_inc(bt_out, 1)
        dve.wait_ge(pa, 1)
        dve.tensor_copy(xn_t[:, :], ps_a[:, 0, :]).then_inc(pa_out_v, 1)
        dve.wait_ge(pa, 10)
        dve.wait_ge(zeroed, 5)
        for b in range(B):
            lo, step = b * SH * 128, 128 + SK
            ins = dve.tensor_copy(v_wide[:, lo:lo + SH * step].rearrange("p (h w) -> p h w", w=step)[:, :, 0:SK],
                                  ps_a[:, 0, b * 128:(b + 1) * 128].rearrange("p (h k) -> p h k", k=SK))
        ins.then_inc(pa_out_v, 1)
        dve.wait_ge(masked, 2 + NE)

        def maxima(b):
            dve.wait_ge(s_ready, b + 1)
            if b >= 2:
                dve.wait_ge(t_ready, 4 * (b - 1))
            lg = att[:, b % 2, :, :]
            dve.scalar_tensor_tensor(out=lg, in0=ps_a[:, :, :].rearrange("p a (c f) -> p (a c) f", c=4),
                                     scalar=float(SK) ** -0.5,
                                     in1=causal[:, :].unsqueeze(1).to_broadcast([128, SH, F]),
                                     op0=ALU.mult, op1=ALU.add).then_inc(s_taken, 1)
            dve.wait_ge(s_taken, b + 1)
            own(dve.tensor_reduce(peak[:, :], lg, AX.X, ALU.max))
            dve.tensor_scalar(negpeak[:, b % 2, :], peak[:, :], -1.0, None, ALU.mult).then_inc(s_shift, 1)

        def scaled(b):
            dve.wait_ge(s_exp, b + 1)
            if b >= 1:
                dve.wait_ge(s_scaled, b)
            own(dve.reciprocal(rtotal[:, :], total[:, b % 2, :]))
            dve.tensor_tensor(att[:, b % 2, :, :], att[:, b % 2, :, :],
                              rtotal[:, :].unsqueeze(2).to_broadcast([128, SH, F]), ALU.mult).then_inc(s_scaled, 1)

        maxima(0)
        dve.wait_ge(s_shift, 1)
        maxima(1)
        scaled(0)
        for b in range(B):
            if b + 1 < B:
                scaled(b + 1)
            if b + 2 < B:
                dve.wait_ge(s_shift, b + 2)
                maxima(b + 2)
            dve.wait_ge(m_ready, b + 1)
            dve.tensor_copy(mixed_t[:, :], ps_b[:, 3, 0:128]).then_inc(m_out, 1)
            dve.wait_ge(o_ready, b + 1)
            dve.tensor_tensor(x_all[:, b, :], ps_b[:, 3, 128:256], x_all[:, b, :], ALU.add).then_inc(o_out, 1)
            dve.wait_ge(o_out, b + 1)
            row_moments(b)
        dve.tensor_scalar(dev[:, :], moments[:, :, 1], LN_EPS, None, ALU.add).then_inc(dev_in, 1)
        dve.wait_ge(powed2, 3)
        normalise(rows_n)
        dve.wait_ge(x_t2, 1)
        dve.tensor_copy(xn_t[:, :], ps_a[:, 0, :]).then_inc(x_t2_out, 1)

        def col(n):
            return g1[n][:, :].unsqueeze(2).to_broadcast([128, B, NE])

        dve.wait_ge(gl_ready, 1)
        own(dve.tensor_copy(g["z"][:, :, :], ps_b[:, 3, 0:B * NE].rearrange("p (b e) -> p b e", b=B)))
        own(dve.tensor_reduce(g1["top"][:, :], g["z"][:, :, :], AX.X, ALU.max))
        dve.tensor_tensor(g["z"][:, :, :], g["z"][:, :, :], col("top"), ALU.subtract).then_inc(gshift, 1)
        dve.wait_ge(gexp, 1)
        own(dve.tensor_reduce(g1["sum"][:, :], g["p"][:, :, :], AX.X, ALU.add))
        own(dve.reciprocal(g1["sum"][:, :], g1["sum"][:, :]))
        own(dve.tensor_tensor(g["left"][:, :, :], g["p"][:, :, :], col("sum"), ALU.mult))
        own(dve.tensor_copy(g["p"][:, :, :], g["left"][:, :, :]))
        for pick in ("one", "two"):
            own(dve.tensor_reduce(g1["best"][:, :], g["left"][:, :, :], AX.X, ALU.max))
            own(dve.tensor_tensor(g["m"][:, :, :], g["left"][:, :, :], col("best"), ALU.is_lt))
            own(dve.scalar_tensor_tensor(out=g["c"][:, :, :], in0=g["m"][:, :, :], scalar=float(NE),
                                         in1=index[:, :, :], op0=ALU.mult, op1=ALU.add))
            own(dve.tensor_reduce(g1["pick"][:, :], g["c"][:, :, :], AX.X, ALU.min))
            own(dve.tensor_tensor(g[pick][:, :, :], index[:, :, :], col("pick"), ALU.is_equal))
            if pick == "one":
                own(dve.scalar_tensor_tensor(out=g["left"][:, :, :], in0=g["one"][:, :, :], scalar=-2.0,
                                             in1=g["left"][:, :, :], op0=ALU.mult, op1=ALU.add))
        own(dve.tensor_tensor(g["one"][:, :, :], g["one"][:, :, :], g["two"][:, :, :], ALU.add))
        dve.tensor_tensor(g["w"][:, :, :], g["one"][:, :, :], g["p"][:, :, :], ALU.mult).then_inc(w_ready, 1)
        dve.wait_ge(w_ready, 1)

        for e in range(NE):
            if e == 4:
                dve.wait_ge(wt_ready, 1)
                dve.tensor_copy(gate_w_t[:, :], ps_b[0:NE, 3, :]).then_inc(wt_out, 1)
            if e == 6:
                dve.wait_ge(bias_ready, 1)
                dve.wait_ge(y_out, e)
                own(dve.tensor_tensor(y[:, :, :].rearrange("p b d -> p (b d)"), ps_b[:, 2, :],
                                      y[:, :, :].rearrange("p b d -> p (b d)"), ALU.add))
            dve.wait_ge(y_ready, e + 1)
            if e:
                dve.wait_ge(y_out, e)
            for b in range(B):
                ins = dve.scalar_tensor_tensor(out=y[:, b, :], in0=ps_b[:, e % 2, b * 128:(b + 1) * 128],
                                               scalar=g["w"][:, b, e:e + 1], in1=(y if e else x_all)[:, b, :],
                                               op0=ALU.mult, op1=ALU.add)
            ins.then_inc(y_out, 1)


_INS = ["x", "ctx_1024", "fside_BxSxS2_0", "mask_Bx1x1xS2_ff0"] + \
    ["L0_xattn_" + n for n in ("Wq", "Wk", "Wv", "Wo", "Wth", "bth", "Wto", "bto", "Wf1", "bf1", "Wf2", "bf2")] + \
    ["L0_attn_" + n for n in ("Wq", "bq", "Wk", "bk", "Wv", "bv", "Wo", "bo")] + \
    ["L0_ffn_" + n for n in ("gate_w", "w1", "b1", "w2", "b2")]


def kernel(**inputs):
    import numpy as np
    import concourse.bacc as bacc
    from concourse.bass_utils import run_bass_kernel_spmd

    nc = bacc.Bacc("TRN2", target_bir_lowering=False, num_devices=1)
    arrays, aps = {}, {}
    for name in _INS:
        array = np.ascontiguousarray(inputs[name])
        arrays["in_" + name] = array
        aps[name] = nc.dram_tensor("in_" + name, array.shape, mybir.dt.from_np(array.dtype), kind="ExternalInput").ap()
    out = nc.dram_tensor("out", (B, F, D), F32, kind="ExternalOutput").ap()
    perceiver(nc, aps, out)
    result = run_bass_kernel_spmd(nc, [arrays], core_ids=[0])
    return result.results[0]["out"]
```
